# Optimizing a Trainium2 kernel written in Bass

```python
import numpy as np
import jax
import jax.numpy as jnp

def _softmax(x, axis=-1):
    return jax.nn.softmax(x, axis=axis)

def _gelu(x):
    return jax.nn.gelu(x, approximate=True)

def _silu(x):
    return jax.nn.silu(x)

def _sigmoid(x):
    return jax.nn.sigmoid(x)

def _layernorm(x, axis=-1, eps=1e-05):
    m = jnp.mean(x, axis=axis, keepdims=True)
    v = jnp.var(x, axis=axis, keepdims=True)
    return (x - m) / jnp.sqrt(v + eps)

def _scatter_add(tgt, idx, src, axis=0):
    return tgt.at[idx].add(src)

def _segment_sum(src, seg, n):
    return jax.ops.segment_sum(src, seg, n)
kernel_name = 'mk_prb_d1_jaxref_r2_8f7a01'

def setup_inputs(seed: int=0):
    np.random.seed(seed)
    _w = jnp.asarray

    def _L0_attn_setup():
        import jax, jax.numpy as jnp
        import numpy as np
        import math
        N_HEADS = 16
        DIM = 512
        B, S = (2, 1024)

        def _split_heads(x, n_heads):
            b, s, d = x.shape
            dh = d // n_heads
            return x.reshape(b, s, n_heads, dh).transpose(0, 2, 1, 3)
        key = jax.random.key(seed)
        ks = jax.random.split(key, 9)
        std = 0.02
        inp = {'query': jax.random.normal(ks[0], (B, S, DIM), dtype=jnp.float32), 'mask': jnp.ones((B, S), dtype=jnp.int64), 'q_w': jax.random.normal(ks[1], (DIM, DIM), dtype=jnp.float32) * std, 'q_b': jnp.zeros((DIM,), dtype=jnp.float32), 'k_w': jax.random.normal(ks[2], (DIM, DIM), dtype=jnp.float32) * std, 'k_b': jnp.zeros((DIM,), dtype=jnp.float32), 'v_w': jax.random.normal(ks[3], (DIM, DIM), dtype=jnp.float32) * std, 'v_b': jnp.zeros((DIM,), dtype=jnp.float32), 'out_w': jax.random.normal(ks[4], (DIM, DIM), dtype=jnp.float32) * std, 'out_b': jnp.zeros((DIM,), dtype=jnp.float32)}
        return inp
    _L0_attn_in = _L0_attn_setup()

    def _L0_ffn_setup():
        import jax, jax.numpy as jnp
        import numpy as np
        D_MODEL = 512
        key = jax.random.key(seed)
        k_x, k_w, k_a1, k_a2 = jax.random.split(key, 4)
        x = jax.random.normal(k_x, (4, 1024, D_MODEL), dtype=jnp.float32)
        weight = jax.random.normal(k_w, (D_MODEL, D_MODEL), dtype=jnp.float32) * 0.02
        aux_weight1 = jax.random.normal(k_a1, (D_MODEL, D_MODEL), dtype=jnp.float32) * 0.02
        aux_weight2 = jax.random.normal(k_a2, (D_MODEL, D_MODEL), dtype=jnp.float32) * 0.02
        bias = jnp.zeros((D_MODEL,), dtype=jnp.float32)
        return {'x': x, 'weight': weight, 'aux_weight1': aux_weight1, 'aux_weight2': aux_weight2, 'bias': bias}
    _L0_ffn_in = _L0_ffn_setup()
    _d = {'L0_attn_query': _L0_attn_in['query'], 'L0_attn_mask': _L0_attn_in['mask'], 'L0_attn_q_w': _L0_attn_in['q_w'], 'L0_attn_q_b': _L0_attn_in['q_b'], 'L0_attn_k_w': _L0_attn_in['k_w'], 'L0_attn_k_b': _L0_attn_in['k_b'], 'L0_attn_v_w': _L0_attn_in['v_w'], 'L0_attn_v_b': _L0_attn_in['v_b'], 'L0_attn_out_w': _L0_attn_in['out_w'], 'L0_attn_out_b': _L0_attn_in['out_b'], 'L0_ffn_weight': _L0_ffn_in['weight'], 'L0_ffn_aux_weight1': _L0_ffn_in['aux_weight1'], 'L0_ffn_aux_weight2': _L0_ffn_in['aux_weight2'], 'L0_ffn_bias': _L0_ffn_in['bias']}
    _x0 = _d['L0_attn_query']
    _d['L0_attn_query'] = jax.random.normal(jax.random.fold_in(jax.random.key(seed), 1), (4, 2048, 512), dtype=_x0.dtype)
    del _x0
    return _d

def reference(L0_attn_query, L0_attn_mask, L0_attn_q_w, L0_attn_q_b, L0_attn_k_w, L0_attn_k_b, L0_attn_v_w, L0_attn_v_b, L0_attn_out_w, L0_attn_out_b, L0_ffn_weight, L0_ffn_aux_weight1, L0_ffn_aux_weight2, L0_ffn_bias):

    def _L0_attn_ref(query, mask, q_w, q_b, k_w, k_b, v_w, v_b, out_w, out_b):
        import jax, jax.numpy as jnp
        import numpy as np
        import math
        N_HEADS = 16
        DIM = 512
        B, S = (2, 1024)

        def _split_heads(x, n_heads):
            b, s, d = x.shape
            dh = d // n_heads
            return x.reshape(b, s, n_heads, dh).transpose(0, 2, 1, 3)
        b, s, d = query.shape
        h = N_HEADS
        dh = d // h
        scale = math.sqrt(dh)
        q = _split_heads(query @ q_w.T + q_b, h) / scale
        k = _split_heads(query @ k_w.T + k_b, h)
        v = _split_heads(query @ v_w.T + v_b, h)
        scores = jnp.einsum('bhqd,bhkd->bhqk', q, k)
        attn = jax.nn.softmax(scores.astype(jnp.float32), axis=-1).astype(query.dtype)
        ctx = jnp.einsum('bhqk,bhkd->bhqd', attn, v)
        ctx = ctx.transpose(0, 2, 1, 3).reshape(b, s, d)
        out = ctx @ out_w.T + out_b
        return out

    def _L0_ffn_ref(x, weight, aux_weight1, aux_weight2, bias):
        import jax, jax.numpy as jnp
        import numpy as np
        D_MODEL = 512
        h = jnp.einsum('btc,cd->btd', x, weight)
        h = jnp.einsum('btc,cd->btd', h, aux_weight1)
        h = jnp.einsum('btc,cd->btd', h, aux_weight2)
        return jnp.tanh(h + bias)
    x = L0_attn_query
    xn = _layernorm(x, axis=-1)
    x = x + _L0_attn_ref(xn, L0_attn_mask, L0_attn_q_w, L0_attn_q_b, L0_attn_k_w, L0_attn_k_b, L0_attn_v_w, L0_attn_v_b, L0_attn_out_w, L0_attn_out_b) + _L0_ffn_ref(xn, L0_ffn_weight, L0_ffn_aux_weight1, L0_ffn_aux_weight2, L0_ffn_bias)
    return x

_drawn_inputs = setup_inputs


def setup_inputs(seed=0):
    import zlib

    import numpy as np

    out = dict(_drawn_inputs(seed))
    spreads = {'L0_attn_q_b': (0.0, 0.8),
     'L0_attn_k_b': (0.0, 2.0),
     'L0_attn_v_b': (0.0, 0.315),
     'L0_attn_out_b': (0.0, 0.1),
     'L0_ffn_bias': (0.0, 0.1)}
    factors = {'L0_attn_q_w': 8.0, 'L0_attn_k_w': 8.0, 'L0_attn_v_w': 8.0}
    for name, (base, spread) in spreads.items():
        noise = np.random.default_rng([zlib.crc32(name.encode()), seed]).standard_normal(out[name].shape)
        drawn = base * np.exp(spread * noise) if base else spread * noise
        out[name] = jnp.asarray(drawn.astype(out[name].dtype))
    for name, factor in factors.items():
        out[name] = (out[name] * factor).astype(out[name].dtype)
    return out
```

```python
from contextlib import ExitStack

import concourse.bass as bass
from concourse import mybir

F32 = mybir.dt.float32
F32R = mybir.dt.float32r
ACT = mybir.ActivationFunctionType
ALU = mybir.AluOpType
AX = mybir.AxisListType

P = 128
BATCH, SEQ, DIM = 4, 2048, 512
HEADS = 16
DH = DIM // HEADS
CT = DIM // P
BLK = 512
JT = BLK // P
BLOCKS = BATCH * SEQ // BLK
TB = SEQ // BLK
EPS = 1e-5
SCALE = float(DH) ** -0.5
DMA = 16
PRIME = 16

KT = SEQ // P
QT = SEQ // P
QB = SEQ // BLK
ALL_HEADS = BATCH * HEADS
GROUP = 4
ROWS = 3 * DH
MROW = ROWS
PROBS = 8
ST_BANKS = 2
SM_PAIRS = 2
PAIRS = QT * SEQ // (2 * BLK)
PLAN = [3, 2, 3, 2, 3, 2, 3, 2, 3, 2, 3, 2, 2, 0, 0, 0]
MAX_KT = 13
POOL_TILES = [0, 1, 3, 4, 6, 7, 9, 10, 12, 13]
POOL_ADDS = len(POOL_TILES) - 1
assert sum(PLAN) == PAIRS and len(PLAN) == KT


def adds_after(kt):
    return max(1, POOL_TILES.index(kt))


def build_weights(nc, ctx, w, dram, keep):
    with ExitStack() as own:
        sb = lambda name, shape, dt=F32: own.enter_context(nc.sbuf_tensor(name, shape, dt))
        sem = lambda name: own.enter_context(nc.semaphore(name))
        raw = {n: sb(f"raw_{n}", [P, CT, DIM]) for n in ("a1", "w", "a2", "q", "k", "v", "o")}
        a1_t, w_t, m1 = sb("a1_t", [P, CT, DIM]), sb("w_t", [P, CT, DIM]), sb("m1", [P, CT, DIM])
        o_hi, o_lo = sb("o_hi", [P, CT, DIM], F32R), sb("o_lo", [P, CT, DIM], F32R)
        bank = own.enter_context(nc.psum_tensor("w_bank", [P, 8, BLK], F32))
        loaded = {n: sem(f"loaded_{n}") for n in raw}
        ident_ready, bank_ready, high_ready, bank_free = sem("ident_ready"), sem("bank_ready"), sem("high_ready"), sem("bank_free")
        small_loaded, wo_stored = sem("small_loaded"), sem("wo_stored")

        split = {"q": 0, "k": 1, "v": 2}
        banks = [("turn", n, c) for n in ("a1", "w") for c in range(CT)]
        banks += [("m1", "m1", c) for c in range(CT)]
        banks += [("turn", n, c) for n in ("q", "k", "v", "o") for c in range(CT)]
        banks += [("ffn", "ffn", c) for c in range(CT)]
        plain = {"a1": a1_t, "w": w_t, "m1": m1}
        high = lambda n: o_hi if n == "o" else keep["w_hi"][:, split.get(n, 3)]
        low = lambda n: o_lo if n == "o" else keep["w_lo"][:, split.get(n, 3)]
        first_m1 = 2 * CT
        splits = [i for i, (_, n, _) in enumerate(banks) if n not in plain]

        block = own.enter_context(nc.Block())

        @block.sync
        def _(sp):
            for n in ("a1", "w", "a2", "q", "k", "v", "o"):
                sp.dma_start(raw[n][:], w[n].rearrange("(r p) c -> p r c", p=P)).then_inc(loaded[n], DMA)
            sp.wait_ge(bank_free, 2 * CT + CT + 4 * CT)
            sp.dma_start(dram["wo_hi"].rearrange("(r p) c -> p r c", p=P), o_hi[:].bitcast(F32)).then_inc(wo_stored, DMA)
            sp.dma_start(dram["wo_lo"].rearrange("(r p) c -> p r c", p=P), o_lo[:].bitcast(F32)).then_inc(wo_stored, DMA)
            sp.wait_ge(wo_stored, 2 * DMA)

        @block.gpsimd
        def _(pool):
            nc.gpsimd.memset(keep["ident"][:], 0.0).then_inc(ident_ready, 1)
            nc.gpsimd.memset(keep["ones"][:], 1.0)
            nc.gpsimd.memset(keep["power"][:], -0.5)
            pool.wait_ge(ident_ready, 1)
            nc.gpsimd.affine_select(out=keep["ident"][:], in_=keep["ident"][:], compare_op=ALU.not_equal, fill=1.0,
                                    base=0, pattern=[[-1, P]], channel_multiplier=1).then_inc(ident_ready, 1)

        @block.scalar
        def _(act):
            act.dma_start(keep["qk_bias"][:, 0], w["q_b"].rearrange("(g p) -> p g", p=P),
                          allow_slow_non_contiguous=True).then_inc(small_loaded, DMA)
            act.dma_start(keep["qk_bias"][:, 1], w["k_b"].rearrange("(g p) -> p g", p=P),
                          allow_slow_non_contiguous=True).then_inc(small_loaded, DMA)
            for i, n in enumerate(("v_b", "ffn_b", "o_b")):
                act.dma_start(keep["row_bias"][:, i], w[n].partition_broadcast(P)).then_inc(small_loaded, DMA)
            for i in splits:
                act.wait_ge(bank_ready, i + 1)
                _, n, c = banks[i]
                nc.scalar.activation(high(n)[:, c], bank[:, i % 8], ACT.Copy).then_inc(high_ready, 1)
            act.wait_ge(small_loaded, 5 * DMA)

        @block.vector
        def _(dve):
            for i, (_, n, c) in enumerate(banks):
                if n in plain:
                    dve.wait_ge(bank_ready, i + 1)
                    nc.vector.tensor_copy(plain[n][:, c], bank[:, i % 8]).then_inc(bank_free, 1)
                else:
                    dve.wait_ge(high_ready, splits.index(i) + 1)
                    nc.vector.tensor_tensor(low(n)[:, c], bank[:, i % 8], high(n)[:, c].bitcast(F32),
                                            ALU.subtract).then_inc(bank_free, 1)

        @block.tensor
        def _(pe):
            pe.wait_ge(ident_ready, 2)
            for i, (kind, n, c) in enumerate(banks):
                if i >= 8:
                    pe.wait_ge(bank_free, i - 7)
                if kind == "turn":
                    if c == 0:
                        pe.wait_ge(loaded[n], DMA)
                    for r in range(CT):
                        last = nc.tensor.transpose(bank[:, i % 8, r * P:(r + 1) * P], raw[n][:, r, c * P:(c + 1) * P],
                                                   keep["ident"][:])
                else:
                    left, right = (a1_t, raw["a2"]) if kind == "m1" else (w_t, m1)
                    if c == 0:
                        pe.wait_ge(bank_free, first_m1 if kind == "m1" else first_m1 + CT)
                        if kind == "m1":
                            pe.wait_ge(loaded["a2"], DMA)
                    for r in range(CT):
                        last = nc.tensor.matmul(bank[:, i % 8], left[:, r, c * P:(c + 1) * P], right[:, r],
                                                start=(r == 0), stop=(r == CT - 1))
                last.then_inc(bank_ready, 1)


def three_passes(nc, out, left_hi, left_lo, right_hi, right_lo):
    for c in range(CT):
        for n, (a, b) in enumerate(((left_hi, right_hi), (left_hi, right_lo), (left_lo, right_hi))):
            last = nc.tensor.matmul(out, a(c), b(c), start=(c == 0 and n == 0), stop=(c == CT - 1 and n == 2))
    return last


def build_project(nc, x, dram, keep):
    with ExitStack() as own:
        sb = lambda name, shape, dt=F32: own.enter_context(nc.sbuf_tensor(name, shape, dt))
        sem = lambda name: own.enter_context(nc.semaphore(name))
        x_in = sb("x_in", [P, 2, JT, DIM])
        stats, mean_var, rstd = sb("stats", [P, JT, 6]), sb("mean_var", [P, JT, 2]), sb("rstd", [P, JT])
        xn = sb("xn", [P, JT, DIM])
        xt_hi, xt_lo = sb("xt_hi", [P, 2, CT, BLK], F32R), sb("xt_lo", [P, 2, CT, BLK], F32R)
        qk_hi, qk_lo = sb("qk_hi", [P, 2, CT, BLK], F32R), sb("qk_lo", [P, 2, CT, BLK], F32R)
        v_out, y_out = sb("v_out", [P, JT, DIM]), sb("y_out", [P, JT, DIM])
        turned = own.enter_context(nc.psum_tensor("turned", [P, CT, BLK], F32))
        RING = 4
        proj = own.enter_context(nc.psum_tensor("proj", [P, RING, BLK], F32))
        x_loaded = [sem("x_loaded0"), sem("x_loaded1")]
        stats_ready, mean_ready, var_ready, rstd_ready = sem("stats_ready"), sem("mean_ready"), sem("var_ready"), sem("rstd_ready")
        xn_ready, turned_ready, xt_hi_ready, xt_lo_ready = sem("xn_ready"), sem("turned_ready"), sem("xt_hi_ready"), sem("xt_lo_ready")
        proj_ready, hi_ready, proj_free = sem("proj_ready"), sem("hi_ready"), sem("proj_free")
        tanh_ready, half_y, y_ready = sem("tanh_ready"), sem("half_y"), sem("y_ready")
        qk_stored = [sem("q_stored"), sem("k_stored")]
        v_stored, y_stored = sem("v_stored"), sem("y_stored")
        UNITS = 2 * CT + 2 * JT

        def pairs(eng, body, ahead):
            with eng.Fori(0, BLOCKS // 2 - 1) as i:
                for par in range(2):
                    body(i * 2 + par, par, True)
            for par in range(2):
                body(BLOCKS - 2 + par, par, par == 0 or not ahead)

        block = own.enter_context(nc.Block())

        @block.sync
        def _(sp):
            tokens = lambda t, n: t[bass.ds(n * BLK, BLK), :].rearrange("(j p) c -> p j c", p=P)
            channels = lambda t, n: t[bass.ds((n // TB) * DIM, DIM), bass.ds((n % TB) * BLK, BLK)].rearrange(
                "(g p) t -> p g t", p=P)
            sp.sem_inc(x_loaded[0], PRIME)
            sp.sem_inc(x_loaded[1], PRIME)
            for s in (*qk_stored, v_stored, y_stored):
                sp.sem_inc(s, PRIME)
            for n in range(2):
                sp.dma_start(x_in[:, n], tokens(x, n)).then_inc(x_loaded[n], DMA)

            def body(n, par, ahead):
                for t, names in enumerate((("q_hi", "q_lo"), ("k_hi", "k_lo"))):
                    sp.wait_ge(proj_free, PRIME + n * UNITS + CT * (t + 1))
                    sp.dma_start(channels(dram[names[0]], n), qk_hi[:, t].bitcast(F32)).then_inc(qk_stored[t], DMA)
                    sp.dma_start(channels(dram[names[1]], n), qk_lo[:, t].bitcast(F32)).then_inc(qk_stored[t], DMA)
                sp.wait_ge(proj_free, PRIME + n * UNITS + 2 * CT + JT)
                sp.dma_start(tokens(dram["v"], n), v_out[:]).then_inc(v_stored, DMA)
                sp.wait_ge(y_ready, n * JT + JT)
                sp.dma_start(tokens(dram["y"], n), y_out[:]).then_inc(y_stored, DMA)
                if ahead:
                    sp.dma_start(x_in[:, par], tokens(x, n + 2)).then_inc(x_loaded[par], DMA)

            with sp.Fori(0, BLOCKS // 2 - 1) as i:
                for par in range(2):
                    body(i * 2 + par, par, True)
            for par in range(2):
                body(BLOCKS - 2 + par, par, False)
            for s in qk_stored:
                sp.wait_ge(s, PRIME + 2 * DMA * BLOCKS)
            sp.wait_ge(v_stored, PRIME + DMA * BLOCKS)
            sp.wait_ge(y_stored, PRIME + DMA * BLOCKS)

        @block.gpsimd
        def _(pool):
            def deviation(n, par):
                pool.wait_ge(var_ready, n + 1)
                nc.gpsimd.tensor_tensor(rstd[:], rstd[:], keep["power"][:], ALU.pow).then_inc(rstd_ready, 1)

            def body(n, par, ahead):
                if ahead:
                    deviation(n + 1, 1 - par)
                for j in range(JT):
                    pool.wait_ge(tanh_ready, n * JT + j + 1)
                    nc.gpsimd.tensor_tensor(y_out[:, j], y_out[:, j], x_in[:, par, j], ALU.add).then_inc(half_y, 1)
                    pool.wait_ge(half_y, n * JT + j + 1)
                    nc.gpsimd.tensor_tensor(y_out[:, j], y_out[:, j], keep["row_bias"][:, 2], ALU.add).then_inc(y_ready, 1)

            deviation(0, 0)
            pairs(pool, body, True)

        @block.scalar
        def _(act):
            act.sem_inc(hi_ready, PRIME)

            def turn_high(n, par):
                for c in range(CT):
                    act.wait_ge(turned_ready, n * CT + c + 1)
                    nc.scalar.activation(xt_hi[:, par, c], turned[:, c], ACT.Copy).then_inc(xt_hi_ready, 1)

            def body(n, par, ahead):
                for t in range(2):
                    act.wait_ge(qk_stored[t], PRIME + n * (2 * DMA))
                    for g in range(CT):
                        u = t * CT + g
                        act.wait_ge(proj_ready, n * UNITS + u + 1)
                        nc.scalar.activation(qk_hi[:, t, g], proj[:, u % RING], ACT.Identity,
                                             bias=keep["qk_bias"][:, t, g:g + 1]).then_inc(hi_ready, 1)
                if ahead:
                    turn_high(n + 1, 1 - par)
                for j in range(JT):
                    act.wait_ge(proj_free, PRIME + n * UNITS + 2 * CT + JT + j + 1)
                    nc.scalar.activation(y_out[:, j], y_out[:, j], ACT.Tanh).then_inc(tanh_ready, 1)

            turn_high(0, 0)
            pairs(act, body, True)

        @block.vector
        def _(dve):
            dve.sem_inc(proj_free, PRIME)
            dve.sem_inc(xn_ready, PRIME)

            def moments(n, par):
                dve.wait_ge(x_loaded[par], PRIME + DMA * (n // 2 + 1))
                for j in range(JT):
                    last = nc.vector.bn_stats(stats[:, j], x_in[:, par, j])
                last.then_inc(stats_ready, 1)

            def aggregate(n):
                for j in range(JT):
                    last = nc.vector.bn_aggr(mean_var[:, j], stats[:, j])
                last.then_inc(mean_ready, 1)
                dve.wait_ge(mean_ready, n + 1)
                nc.vector.tensor_scalar(rstd[:], mean_var[:, :, 1], EPS, None, ALU.add).then_inc(var_ready, 1)

            def normalize(n, par):
                dve.wait_ge(rstd_ready, n + 1)
                for j in range(JT):
                    last = nc.vector.tensor_scalar(xn[:, j], x_in[:, par, j], mean_var[:, j, 0:1], rstd[:, j:j + 1],
                                                   ALU.subtract, ALU.mult)
                last.then_inc(xn_ready, 1)

            def turn_low(n, par):
                for c in range(CT):
                    dve.wait_ge(xt_hi_ready, n * CT + c + 1)
                    nc.vector.tensor_tensor(xt_lo[:, par, c], turned[:, c], xt_hi[:, par, c].bitcast(F32),
                                            ALU.subtract).then_inc(xt_lo_ready, 1)

            def body(n, par, ahead):
                if ahead:
                    moments(n + 1, 1 - par)
                for t in range(2):
                    for g in range(CT):
                        u = t * CT + g
                        if u == 0 and ahead:
                            dve.wait_ge(stats_ready, n + 2)
                        dve.wait_ge(hi_ready, PRIME + n * (2 * CT) + u + 1)
                        nc.vector.scalar_tensor_tensor(qk_lo[:, t, g], proj[:, u % RING], keep["qk_bias"][:, t, g:g + 1],
                                                       qk_hi[:, t, g].bitcast(F32), ALU.add,
                                                       ALU.subtract).then_inc(proj_free, 1)
                        if u == 0 and ahead:
                            aggregate(n + 1)
                    if t == 0 and ahead:
                        normalize(n + 1, 1 - par)
                if ahead:
                    turn_low(n + 1, 1 - par)
                for j in range(JT):
                    if j == 0:
                        dve.wait_ge(v_stored, PRIME + n * DMA)
                    u = 2 * CT + j
                    dve.wait_ge(proj_ready, n * UNITS + u + 1)
                    nc.vector.tensor_tensor(v_out[:, j], proj[:, u % RING], keep["row_bias"][:, 0],
                                            ALU.add).then_inc(proj_free, 1)
                for j in range(JT):
                    if j == 0:
                        dve.wait_ge(y_stored, PRIME + n * DMA)
                    u = 2 * CT + JT + j
                    dve.wait_ge(proj_ready, n * UNITS + u + 1)
                    nc.vector.tensor_tensor(y_out[:, j], proj[:, u % RING], keep["row_bias"][:, 1],
                                            ALU.add).then_inc(proj_free, 1)

            moments(0, 0)
            dve.wait_ge(stats_ready, 1)
            aggregate(0)
            normalize(0, 0)
            turn_low(0, 0)
            pairs(dve, body, True)

        @block.tensor
        def _(pe):
            w_hi, w_lo = keep["w_hi"], keep["w_lo"]

            def turn(n, par):
                pe.wait_ge(xn_ready, PRIME + n + 1)
                for c in range(CT):
                    for j in range(JT):
                        last = nc.tensor.transpose(turned[:, c, j * P:(j + 1) * P], xn[:, j, c * P:(c + 1) * P],
                                                   keep["ident"][:])
                    last.then_inc(turned_ready, 1)

            def body(n, par, ahead):
                pe.wait_ge(xt_lo_ready, n * CT + CT)
                x_hi = lambda c: xt_hi[:, par, c]
                x_lo = lambda c: xt_lo[:, par, c]
                for u in range(2 * CT):
                    t, g = divmod(u, CT)
                    pe.wait_ge(proj_free, PRIME + n * UNITS + u - RING + 1)
                    three_passes(nc, proj[:, u % RING], lambda c: w_hi[:, t, c, g * P:(g + 1) * P],
                                 lambda c: w_lo[:, t, c, g * P:(g + 1) * P], x_hi, x_lo).then_inc(proj_ready, 1)
                if ahead:
                    turn(n + 1, 1 - par)
                for u in range(2 * CT, UNITS):
                    t, j = divmod(u - 2 * CT, JT)
                    pe.wait_ge(proj_free, PRIME + n * UNITS + u - RING + 1)
                    three_passes(nc, proj[:, u % RING], lambda c: x_hi(c)[:, j * P:(j + 1) * P],
                                 lambda c: x_lo(c)[:, j * P:(j + 1) * P], lambda c: w_hi[:, 2 + t, c],
                                 lambda c: w_lo[:, 2 + t, c]).then_inc(proj_ready, 1)

            turn(0, 0)
            pairs(pe, body, True)


def build_attend(nc, dram):
    with ExitStack() as own:
        sb = lambda name, shape, dt=F32: own.enter_context(nc.sbuf_tensor(name, shape, dt))
        ps = lambda name, shape: own.enter_context(nc.psum_tensor(name, shape, F32))
        sem = lambda name: own.enter_context(nc.semaphore(name))
        q_st = [sb(f"q_stack{r}", [P, SEQ], F32R) for r in range(GROUP)]
        k_st = [sb(f"k_stack{r}", [P, SEQ], F32R) for r in range(GROUP)]
        v_sb = [sb(f"v_head{r}", [P, KT, DH]) for r in range(GROUP)]
        probs = [sb(f"probs{s}", [P, SEQ]) for s in range(PROBS)]
        pool_sum = [sb(f"pool_sum{s}", [P, SEQ]) for s in range(2)]
        ones, ident = sb("ones_att", [P, DH]), sb("ident_att", [P, P])
        pair_max, row_max = sb("pair_max", [P, PAIRS]), sb("row_max", [P, QT])
        max_row = sb("max_row", [QT, P], F32R)
        rsum = sb("rsum", [P, BLK])
        ctx_out = [sb(f"ctx_out{s}", [P, BLK]) for s in range(2)]
        st_bank = ps("st_bank", [P, ST_BANKS, BLK])
        sm_bank = ps("sm_bank", [P, SM_PAIRS, 2, BLK])
        pv_bank = ps("pv_bank", [P, BLK])
        sum_bank = ps("sum_bank", [P, BLK])
        consts_ready, ident_zero = sem("consts_ready"), sem("ident_zero")
        head_loaded = [sem(f"head_loaded{r}") for r in range(GROUP)]
        row_loaded = [sem(f"row_loaded{r}") for r in range(GROUP)]
        scores_ready, probs_ready, tile_used = sem("scores_ready"), sem("probs_ready"), sem("tile_used")
        pairs_ready, pairs_read = sem("pairs_ready"), sem("pairs_read")
        row_max_ready, turned_ready, max_row_ready = sem("row_max_ready"), sem("max_turned"), sem("max_row_ready")
        pool_added, sums_ready, recip_ready, context_ready = sem("pool_added"), sem("sums_ready"), sem("recip_ready"), sem("context_ready")
        context_stored = [sem("context_stored0"), sem("context_stored1")]
        HEAD_DMAS = 7
        CTX_DMAS = QB

        def heads(eng, body):
            with eng.Fori(0, ALL_HEADS // GROUP - 1) as i:
                for r in range(GROUP):
                    body(i * GROUP + r, r, 2)
            for r in range(GROUP):
                body(ALL_HEADS - GROUP + r, r, min(2, GROUP - 1 - r))

        pairs_before = [sum(PLAN[:kt]) for kt in range(KT)]

        block = own.enter_context(nc.Block())

        @block.sync
        def _(sp):
            for s in (*head_loaded, *row_loaded, *context_stored):
                sp.sem_inc(s, PRIME)

            def load(h, r):
                rows = lambda t: dram[t][bass.ds(h * DH, DH), :]
                for i, t in enumerate(("q_hi", "q_lo", "q_hi")):
                    sp.dma_start(q_st[r][i * DH:(i + 1) * DH, :].bitcast(F32), rows(t)).then_inc(head_loaded[r], DMA)
                for i, t in enumerate(("k_hi", "k_hi", "k_lo")):
                    sp.dma_start(k_st[r][i * DH:(i + 1) * DH, :].bitcast(F32), rows(t)).then_inc(head_loaded[r], DMA)
                v_rows = dram["v"][bass.ds((h // HEADS) * SEQ, SEQ), bass.ds((h % HEADS) * DH, DH)]
                sp.dma_start(v_sb[r][:], v_rows.rearrange("(t p) d -> p t d", p=P)).then_inc(head_loaded[r], DMA)

            def load_row(h, r):
                sp.wait_ge(max_row_ready, h + 1)
                sp.dma_start(q_st[r][MROW:MROW + 1, :].bitcast(F32), max_row[:].bitcast(F32)).then_inc(row_loaded[r], DMA)

            def store(h, r):
                sp.wait_ge(context_ready, PRIME + h + 1)
                for q in range(QB):
                    sp.dma_start(dram["ctx"][bass.ds(h * DH, DH), q * BLK:(q + 1) * BLK],
                                 ctx_out[r % 2][q * DH:(q + 1) * DH, :]).then_inc(context_stored[r % 2], DMA)

            for h in range(3):
                load(h, h)
            load_row(0, 0)

            def body(h, r, more):
                if more >= 1:
                    load_row(h + 1, (r + 1) % GROUP)
                store(h, r)
                if more >= 2 and not (isinstance(h, int) and h + 3 >= ALL_HEADS):
                    load(h + 3, (r + 3) % GROUP)

            heads(sp, body)
            for s in context_stored:
                sp.wait_ge(s, PRIME + CTX_DMAS * DMA * ALL_HEADS // 2)

        @block.gpsimd
        def _(pool):
            pool.sem_inc(pool_added, PRIME)
            nc.gpsimd.memset(ident[:], 0.0).then_inc(ident_zero, 1)
            nc.gpsimd.memset(ones[:], 1.0).then_inc(consts_ready, 1)
            pool.wait_ge(ident_zero, 1)
            nc.gpsimd.affine_select(out=ident[:], in_=ident[:], compare_op=ALU.not_equal, fill=1.0, base=0,
                                    pattern=[[-1, P]], channel_multiplier=1).then_inc(consts_ready, 1)

            def body(h, r, more):
                total = pool_sum[r % 2]
                for i, kt in enumerate(POOL_TILES[1:]):
                    if i == 0:
                        pool.wait_ge(sums_ready, PRIME + h - 1)
                    pool.wait_ge(probs_ready, PRIME + h * (KT * QB) + QB * (kt + 1))
                    if i == 0:
                        one = probs[POOL_TILES[0] % PROBS]
                    else:
                        pool.wait_ge(pool_added, PRIME + h * POOL_ADDS + i)
                        one = total
                    nc.gpsimd.tensor_tensor(total[:], one[:], probs[kt % PROBS][:], ALU.add).then_inc(pool_added, 1)

            heads(pool, body)

        @block.scalar
        def _(act):
            act.sem_inc(probs_ready, PRIME)

            def exps(h, kt):
                for q in range(QB):
                    if q == 0:
                        act.wait_ge(tile_used, PRIME + h * KT + kt - PROBS + 1)
                        old, back = ((kt - PROBS), 0) if kt >= PROBS else (kt - PROBS + KT, 1)
                        if old in POOL_TILES:
                            act.wait_ge(pool_added, PRIME + h * POOL_ADDS - back * POOL_ADDS + adds_after(old))
                    act.wait_ge(scores_ready, h * (KT * QB) + kt * QB + q + 1)
                    nc.scalar.activation(probs[kt % PROBS][:, q * BLK:(q + 1) * BLK], st_bank[:, q % ST_BANKS],
                                         ACT.Exp, scale=SCALE).then_inc(probs_ready, 1)

            exps(0, 0)

            def body(h, r, more):
                for kt in range(1, KT):
                    exps(h, kt)
                if more:
                    exps(h + 1, 0)

            heads(act, body)

        @block.vector
        def _(dve):
            dve.sem_inc(pairs_read, PRIME)
            dve.sem_inc(context_ready, PRIME)

            def maxima(s, kt):
                for k in range(pairs_before[kt], pairs_before[kt] + PLAN[kt]):
                    dve.wait_ge(pairs_ready, s * PAIRS + k + 1)
                    if k == 0:
                        dve.wait_ge(row_max_ready, PRIME + s)
                    nc.vector.tensor_reduce(pair_max[:, k:k + 1], sm_bank[:, k % SM_PAIRS], AX.XY,
                                            ALU.max).then_inc(pairs_read, 1)

            def max_to_row(s):
                dve.wait_ge(pairs_read, PRIME + s * PAIRS + PAIRS)
                nc.vector.tensor_reduce(row_max[:], pair_max[:].rearrange("p (q two) -> p q two", two=2), AX.X,
                                        ALU.max).then_inc(row_max_ready, 1)
                dve.wait_ge(turned_ready, s + 1)
                nc.vector.tensor_scalar(max_row[:], sm_bank[0:QT, 0, 0, 0:P], -1.0, None,
                                        ALU.mult).then_inc(max_row_ready, 1)

            def context(h, r):
                dve.wait_ge(sums_ready, PRIME + h + 1)
                nc.vector.reciprocal(rsum[:], sum_bank[:]).then_inc(recip_ready, 1)
                dve.wait_ge(recip_ready, h + 1)
                dve.wait_ge(context_stored[r % 2], PRIME + (h // 2) * (CTX_DMAS * DMA))
                nc.vector.tensor_tensor(ctx_out[r % 2][:], pv_bank[:], rsum[:], ALU.mult).then_inc(context_ready, 1)

            dve.sem_inc(row_max_ready, PRIME)
            for r in range(GROUP):
                nc.vector.memset(k_st[r][MROW:MROW + 1, :].bitcast(F32), 1.0).then_inc(consts_ready, 1)
            for kt in range(KT):
                maxima(0, kt)
            max_to_row(0)
            maxima(1, 0)

            def body(h, r, more):
                for kt in range(1, KT):
                    if more >= 1:
                        if kt == MAX_KT:
                            max_to_row(h + 1)
                        maxima(h + 1, kt)
                if more >= 2:
                    maxima(h + 2, 0)
                context(h, r)

            heads(dve, body)

        @block.tensor
        def _(pe):
            pe.sem_inc(tile_used, PRIME)
            pe.sem_inc(sums_ready, PRIME)
            pe.wait_ge(consts_ready, 2 + GROUP)

            def max_pair(s, r, k):
                q, half = divmod(k, 2)
                if k == 0:
                    pe.wait_ge(head_loaded[r], PRIME + (s // GROUP) * (HEAD_DMAS * DMA) + HEAD_DMAS * DMA)
                    if not (isinstance(s, int) and s == 0):
                        pe.wait_ge(max_row_ready, s)
                pe.wait_ge(pairs_read, PRIME + s * PAIRS + k - SM_PAIRS + 1)
                for b in range(2):
                    keys = (half * 2 + b) * BLK
                    last = nc.tensor.matmul(sm_bank[:, k % SM_PAIRS, b], q_st[r][0:ROWS, q * P:(q + 1) * P],
                                            k_st[r][0:ROWS, keys:keys + BLK], start=True, stop=True)
                last.then_inc(pairs_ready, 1)

            def scores(h, r, kt, q):
                if kt == 0 and q == 0:
                    pe.wait_ge(row_loaded[r], PRIME + (h // GROUP) * DMA + DMA)
                pe.wait_ge(probs_ready, PRIME + h * (KT * QB) + kt * QB + q - ST_BANKS + 1)
                nc.tensor.matmul(st_bank[:, q % ST_BANKS], k_st[r][0:ROWS + 1, kt * P:(kt + 1) * P],
                                 q_st[r][0:ROWS + 1, q * BLK:(q + 1) * BLK], start=True,
                                 stop=True).then_inc(scores_ready, 1)

            def spread(bank, left, right, start, stop):
                for q in range(QB):
                    last = nc.tensor.matmul(bank[q * DH:(q + 1) * DH, :], left, right[:, q * BLK:(q + 1) * BLK],
                                            start=start, stop=stop)
                return last

            def use(h, r, kt):
                if kt == 0:
                    pe.wait_ge(context_ready, PRIME + h)
                pe.wait_ge(probs_ready, PRIME + h * (KT * QB) + QB * (kt + 1))
                tile = probs[kt % PROBS]
                last = spread(pv_bank, v_sb[r][:, kt], tile, kt == 0, kt == KT - 1)
                if kt not in POOL_TILES:
                    first = all(t in POOL_TILES for t in range(kt))
                    last = spread(sum_bank, ones[:], tile, first, False)
                last.then_inc(tile_used, 1)
                if kt == KT - 1:
                    pe.wait_ge(pool_added, PRIME + h * POOL_ADDS + POOL_ADDS)
                    spread(sum_bank, ones[:], pool_sum[r % 2], False, True).then_inc(sums_ready, 1)

            def step(h, r, kt, s, sr, with_max):
                order = list(range(pairs_before[kt], pairs_before[kt] + PLAN[kt])) if with_max else []
                for q in range(QB):
                    if order:
                        max_pair(s, sr, order.pop(0))
                    scores(h, r, kt, q)

            def turn_max(s):
                pe.wait_ge(row_max_ready, PRIME + s + 1)
                nc.tensor.transpose(sm_bank[0:QT, 0, 0, 0:P], row_max[:], ident[:]).then_inc(turned_ready, 1)

            for k in range(PAIRS):
                max_pair(0, 0, k)
            turn_max(0)
            step(0, 0, 0, 1, 1, True)

            def body(h, r, more):
                r1, r2 = (r + 1) % GROUP, (r + 2) % GROUP
                for kt in range(1, KT):
                    step(h, r, kt, h + 1, r1, more >= 1)
                    use(h, r, kt - 1)
                    if kt == MAX_KT and more >= 1:
                        turn_max(h + 1)
                if more >= 1:
                    step(h + 1, r1, 0, h + 2, r2, more >= 2)
                use(h, r, KT - 1)

            heads(pe, body)


def build_output(nc, dram, out):
    with ExitStack() as own:
        sb = lambda name, shape, dt=F32: own.enter_context(nc.sbuf_tensor(name, shape, dt))
        sem = lambda name: own.enter_context(nc.semaphore(name))
        wo_hi, wo_lo = sb("wo_hi_sb", [P, CT, DIM], F32R), sb("wo_lo_sb", [P, CT, DIM], F32R)
        ctx_in = [sb(f"ctx_in{s}", [P, CT, BLK]) for s in range(2)]
        y_in = [sb(f"y_in{s}", [P, JT, DIM]) for s in range(2)]
        ctx_hi = [sb(f"ctx_hi{s}", [P, CT, BLK], F32R) for s in range(2)]
        ctx_lo = [sb(f"ctx_lo{s}", [P, CT, BLK], F32R) for s in range(2)]
        res = [sb(f"res{s}", [P, JT, DIM]) for s in range(2)]
        RING = 8
        bank = own.enter_context(nc.psum_tensor("out_bank", [P, RING, BLK], F32))
        w_loaded = sem("wo_loaded")
        ctx_loaded, y_loaded = [sem("ctx_loaded0"), sem("ctx_loaded1")], [sem("y_loaded0"), sem("y_loaded1")]
        hi_ready, lo_ready, bank_ready, res_ready = sem("ctx_hi_ready"), sem("ctx_lo_ready"), sem("out_bank_ready"), sem("res_ready")
        stored = [sem("stored0"), sem("stored1")]

        def pairs(eng, body):
            with eng.Fori(0, BLOCKS // 2 - 1) as i:
                for par in range(2):
                    body(i * 2 + par, par, True)
            for par in range(2):
                body(BLOCKS - 2 + par, par, False)

        block = own.enter_context(nc.Block())
        tokens = lambda t, n: t[bass.ds(n * BLK, BLK), :].rearrange("(j p) c -> p j c", p=P)

        @block.sync
        def _(sp):
            sp.dma_start(wo_hi[:].bitcast(F32), dram["wo_hi"].rearrange("(r p) c -> p r c", p=P)).then_inc(w_loaded, DMA)
            sp.dma_start(wo_lo[:].bitcast(F32), dram["wo_lo"].rearrange("(r p) c -> p r c", p=P)).then_inc(w_loaded, DMA)
            for s in stored:
                sp.sem_inc(s, PRIME)

            def load(n, par):
                src = dram["ctx"][bass.ds((n // TB) * DIM, DIM), bass.ds((n % TB) * BLK, BLK)]
                sp.dma_start(ctx_in[par][:], src.rearrange("(c p) t -> p c t", p=P)).then_inc(ctx_loaded[par], DMA)
                sp.dma_start(y_in[par][:], tokens(dram["y"], n)).then_inc(y_loaded[par], DMA)

            for n in range(2):
                load(n, n)

            def body(n, par, ahead):
                sp.wait_ge(res_ready, PRIME + n * JT + JT)
                sp.dma_start(tokens(out, n), res[par][:]).then_inc(stored[par], DMA)
                if ahead:
                    load(n + 2, par)

            pairs(sp, body)
            for s in stored:
                sp.wait_ge(s, PRIME + DMA * BLOCKS // 2)

        @block.scalar
        def _(act):
            act.wait_ge(w_loaded, 2 * DMA)

            def body(n, par, ahead):
                act.wait_ge(ctx_loaded[par], (n // 2) * DMA + DMA)
                act.wait_ge(res_ready, PRIME + n * JT - JT)
                nc.scalar.activation(ctx_hi[par][:], ctx_in[par][:], ACT.Copy).then_inc(hi_ready, 1)

            pairs(act, body)

        @block.vector
        def _(dve):
            dve.sem_inc(res_ready, PRIME)

            def low(n, par):
                dve.wait_ge(hi_ready, n + 1)
                nc.vector.tensor_tensor(ctx_lo[par][:], ctx_in[par][:], ctx_hi[par][:].bitcast(F32),
                                        ALU.subtract).then_inc(lo_ready, 1)

            low(0, 0)

            def body(n, par, ahead):
                if ahead or par == 0:
                    low(n + 1, 1 - par)
                dve.wait_ge(y_loaded[par], (n // 2) * DMA + DMA)
                dve.wait_ge(stored[par], PRIME + (n // 2) * DMA)
                for j in range(JT):
                    dve.wait_ge(bank_ready, n * JT + j + 1)
                    nc.vector.tensor_tensor(res[par][:, j], bank[:, JT * par + j], y_in[par][:, j],
                                            ALU.add).then_inc(res_ready, 1)

            pairs(dve, body)

        @block.tensor
        def _(pe):
            pe.wait_ge(w_loaded, 2 * DMA)

            def body(n, par, ahead):
                pe.wait_ge(lo_ready, n + 1)
                for j in range(JT):
                    pe.wait_ge(res_ready, PRIME + n * JT + j - RING + 1)
                    three_passes(nc, bank[:, JT * par + j], lambda c: ctx_hi[par][:, c, j * P:(j + 1) * P],
                                 lambda c: ctx_lo[par][:, c, j * P:(j + 1) * P], lambda c: wo_hi[:, c],
                                 lambda c: wo_lo[:, c]).then_inc(bank_ready, 1)

            pairs(pe, body)


def build_program(nc, x, w, out):
    x, out = x.flatten_outer_dims(), out.flatten_outer_dims()
    scratch = lambda name, shape: nc.dram_tensor(name, shape, F32, kind="Internal").ap()
    dram = {n: scratch(f"s_{n}", [BATCH * DIM, SEQ]) for n in ("q_hi", "q_lo", "k_hi", "k_lo", "ctx")}
    dram |= {n: scratch(f"s_{n}", [BATCH * SEQ, DIM]) for n in ("v", "y")}
    dram |= {n: scratch(f"s_{n}", [DIM, DIM]) for n in ("wo_hi", "wo_lo")}
    with ExitStack() as ctx:
        sb = lambda name, shape, dt=F32: ctx.enter_context(nc.sbuf_tensor(name, shape, dt))
        keep = {
            "ident": sb("ident", [P, P]), "ones": sb("ones", [P, DH]), "power": sb("power", [P, JT]),
            "qk_bias": sb("qk_bias", [P, 2, CT]), "row_bias": sb("row_bias", [P, 3, DIM]),
            "w_hi": sb("w_hi", [P, 4, CT, DIM], F32R), "w_lo": sb("w_lo", [P, 4, CT, DIM], F32R),
        }
        build_weights(nc, ctx, w, dram, keep)
        build_project(nc, x, dram, keep)
    build_attend(nc, dram)
    build_output(nc, dram, out)


_NAMES = {
    "x": "L0_attn_query", "q": "L0_attn_q_w", "q_b": "L0_attn_q_b", "k": "L0_attn_k_w", "k_b": "L0_attn_k_b",
    "v": "L0_attn_v_w", "v_b": "L0_attn_v_b", "o": "L0_attn_out_w", "o_b": "L0_attn_out_b",
    "w": "L0_ffn_weight", "a1": "L0_ffn_aux_weight1", "a2": "L0_ffn_aux_weight2", "ffn_b": "L0_ffn_bias",
}


def kernel(**inputs):
    import numpy as np
    import concourse.bacc as bacc
    from concourse.bass_utils import run_bass_kernel_spmd

    nc = bacc.Bacc("TRN2", target_bir_lowering=False, num_devices=1)
    arrays, given = {}, {}
    for short, name in _NAMES.items():
        a = np.ascontiguousarray(inputs[name])
        arrays[f"in_{short}"] = a
        given[short] = nc.dram_tensor(f"in_{short}", a.shape, mybir.dt.from_np(a.dtype), kind="ExternalInput").ap()
    x = given.pop("x")
    out = nc.dram_tensor("out_0", x.shape, F32, kind="ExternalOutput").ap()
    build_program(nc, x, given, out)
    r = run_bass_kernel_spmd(nc, [arrays], core_ids=[0])
    return r.results[0]["out_0"]
```

```python
from contextlib import ExitStack

import concourse.bass as bass
from concourse import mybir

F32 = mybir.dt.float32
F32R = mybir.dt.float32r
ACT = mybir.ActivationFunctionType
ALU = mybir.AluOpType
AX = mybir.AxisListType

P = 128
BATCH, SEQ, DIM = 4, 2048, 512
HEADS = 16
DH = DIM // HEADS
CT = DIM // P
BLK = 512
JT = BLK // P
BLOCKS = BATCH * SEQ // BLK
TB = SEQ // BLK
EPS = 1e-5
SCALE = float(DH) ** -0.5
DMA = 16
PRIME = 16

KT = SEQ // P
QT = SEQ // P
QB = SEQ // BLK
ALL_HEADS = BATCH * HEADS
GROUP = 4
ROWS = 3 * DH
MROW = ROWS
PROBS = 8
ST_BANKS = 3
SM_BANKS = 3
UNITS = KT * QB
PLAN = [5] * 12 + [4, 0, 0, 0]
MAX_KT = 13
POOL_TILES = [0, 1, 3, 4, 6, 7, 9, 10, 12, 13]
POOL_ADDS = len(POOL_TILES) - 1
assert sum(PLAN) == UNITS and len(PLAN) == KT


def adds_after(kt):
    return max(1, POOL_TILES.index(kt))


def build_weights(nc, ctx, w, dram, keep):
    with ExitStack() as own:
        sb = lambda name, shape, dt=F32: own.enter_context(nc.sbuf_tensor(name, shape, dt))
        sem = lambda name: own.enter_context(nc.semaphore(name))
        raw = {n: sb(f"raw_{n}", [P, CT, DIM]) for n in ("a1", "w", "a2", "q", "k", "v", "o")}
        a1_t, w_t, m1 = sb("a1_t", [P, CT, DIM]), sb("w_t", [P, CT, DIM]), sb("m1", [P, CT, DIM])
        o_hi, o_lo = sb("o_hi", [P, CT, DIM], F32R), sb("o_lo", [P, CT, DIM], F32R)
        bank = own.enter_context(nc.psum_tensor("w_bank", [P, 8, BLK], F32))
        loaded = {n: sem(f"loaded_{n}") for n in raw}
        ident_ready, bank_ready, high_ready, bank_free = sem("ident_ready"), sem("bank_ready"), sem("high_ready"), sem("bank_free")
        small_loaded, wo_stored = sem("small_loaded"), sem("wo_stored")

        split = {"q": 0, "k": 1, "v": 2}
        banks = [("turn", n, c) for n in ("a1", "w") for c in range(CT)]
        banks += [("m1", "m1", c) for c in range(CT)]
        banks += [("turn", n, c) for n in ("q", "k", "v", "o") for c in range(CT)]
        banks += [("ffn", "ffn", c) for c in range(CT)]
        plain = {"a1": a1_t, "w": w_t, "m1": m1}
        high = lambda n: o_hi if n == "o" else keep["w_hi"][:, split.get(n, 3)]
        low = lambda n: o_lo if n == "o" else keep["w_lo"][:, split.get(n, 3)]
        first_m1 = 2 * CT
        splits = [i for i, (_, n, _) in enumerate(banks) if n not in plain]

        block = own.enter_context(nc.Block())

        @block.sync
        def _(sp):
            for n in ("a1", "w", "a2", "q", "k", "v", "o"):
                sp.dma_start(raw[n][:], w[n].rearrange("(r p) c -> p r c", p=P)).then_inc(loaded[n], DMA)
            sp.wait_ge(bank_free, 2 * CT + CT + 4 * CT)
            sp.dma_start(dram["wo_hi"].rearrange("(r p) c -> p r c", p=P), o_hi[:].bitcast(F32)).then_inc(wo_stored, DMA)
            sp.dma_start(dram["wo_lo"].rearrange("(r p) c -> p r c", p=P), o_lo[:].bitcast(F32)).then_inc(wo_stored, DMA)
            sp.wait_ge(wo_stored, 2 * DMA)

        @block.gpsimd
        def _(pool):
            nc.gpsimd.memset(keep["ident"][:], 0.0).then_inc(ident_ready, 1)
            nc.gpsimd.memset(keep["ones"][:], 1.0)
            nc.gpsimd.memset(keep["power"][:], -0.5)
            pool.wait_ge(ident_ready, 1)
            nc.gpsimd.affine_select(out=keep["ident"][:], in_=keep["ident"][:], compare_op=ALU.not_equal, fill=1.0,
                                    base=0, pattern=[[-1, P]], channel_multiplier=1).then_inc(ident_ready, 1)

        @block.scalar
        def _(act):
            act.dma_start(keep["qk_bias"][:, 0], w["q_b"].rearrange("(g p) -> p g", p=P),
                          allow_slow_non_contiguous=True).then_inc(small_loaded, DMA)
            act.dma_start(keep["qk_bias"][:, 1], w["k_b"].rearrange("(g p) -> p g", p=P),
                          allow_slow_non_contiguous=True).then_inc(small_loaded, DMA)
            for i, n in enumerate(("v_b", "ffn_b", "o_b")):
                act.dma_start(keep["row_bias"][:, i], w[n].partition_broadcast(P)).then_inc(small_loaded, DMA)
            for i in splits:
                act.wait_ge(bank_ready, i + 1)
                _, n, c = banks[i]
                nc.scalar.activation(high(n)[:, c], bank[:, i % 8], ACT.Copy).then_inc(high_ready, 1)
            act.wait_ge(small_loaded, 5 * DMA)

        @block.vector
        def _(dve):
            for i, (_, n, c) in enumerate(banks):
                if n in plain:
                    dve.wait_ge(bank_ready, i + 1)
                    nc.vector.tensor_copy(plain[n][:, c], bank[:, i % 8]).then_inc(bank_free, 1)
                else:
                    dve.wait_ge(high_ready, splits.index(i) + 1)
                    nc.vector.tensor_tensor(low(n)[:, c], bank[:, i % 8], high(n)[:, c].bitcast(F32),
                                            ALU.subtract).then_inc(bank_free, 1)

        @block.tensor
        def _(pe):
            pe.wait_ge(ident_ready, 2)
            for i, (kind, n, c) in enumerate(banks):
                if i >= 8:
                    pe.wait_ge(bank_free, i - 7)
                if kind == "turn":
                    if c == 0:
                        pe.wait_ge(loaded[n], DMA)
                    for r in range(CT):
                        last = nc.tensor.transpose(bank[:, i % 8, r * P:(r + 1) * P], raw[n][:, r, c * P:(c + 1) * P],
                                                   keep["ident"][:])
                else:
                    left, right = (a1_t, raw["a2"]) if kind == "m1" else (w_t, m1)
                    if c == 0:
                        pe.wait_ge(bank_free, first_m1 if kind == "m1" else first_m1 + CT)
                        if kind == "m1":
                            pe.wait_ge(loaded["a2"], DMA)
                    for r in range(CT):
                        last = nc.tensor.matmul(bank[:, i % 8], left[:, r, c * P:(c + 1) * P], right[:, r],
                                                start=(r == 0), stop=(r == CT - 1))
                last.then_inc(bank_ready, 1)


def three_passes(nc, out, left_hi, left_lo, right_hi, right_lo):
    for c in range(CT):
        for n, (a, b) in enumerate(((left_hi, right_hi), (left_hi, right_lo), (left_lo, right_hi))):
            last = nc.tensor.matmul(out, a(c), b(c), start=(c == 0 and n == 0), stop=(c == CT - 1 and n == 2))
    return last


def build_project(nc, x, dram, keep):
    with ExitStack() as own:
        sb = lambda name, shape, dt=F32: own.enter_context(nc.sbuf_tensor(name, shape, dt))
        sem = lambda name: own.enter_context(nc.semaphore(name))
        x_in = sb("x_in", [P, 2, JT, DIM])
        stats, mean_var, rstd = sb("stats", [P, JT, 6]), sb("mean_var", [P, JT, 2]), sb("rstd", [P, JT])
        xn = sb("xn", [P, JT, DIM])
        xt_hi, xt_lo = sb("xt_hi", [P, 2, CT, BLK], F32R), sb("xt_lo", [P, 2, CT, BLK], F32R)
        qk_hi, qk_lo = sb("qk_hi", [P, 2, CT, BLK], F32R), sb("qk_lo", [P, 2, CT, BLK], F32R)
        v_out, y_out = sb("v_out", [P, JT, DIM]), sb("y_out", [P, JT, DIM])
        turned = own.enter_context(nc.psum_tensor("turned", [P, CT, BLK], F32))
        RING = 4
        proj = own.enter_context(nc.psum_tensor("proj", [P, RING, BLK], F32))
        x_loaded = [sem("x_loaded0"), sem("x_loaded1")]
        stats_ready, mean_ready, var_ready, rstd_ready = sem("stats_ready"), sem("mean_ready"), sem("var_ready"), sem("rstd_ready")
        xn_ready, turned_ready, xt_hi_ready, xt_lo_ready = sem("xn_ready"), sem("turned_ready"), sem("xt_hi_ready"), sem("xt_lo_ready")
        proj_ready, hi_ready, proj_free = sem("proj_ready"), sem("hi_ready"), sem("proj_free")
        tanh_ready, half_y, y_ready = sem("tanh_ready"), sem("half_y"), sem("y_ready")
        qk_stored = [sem("q_stored"), sem("k_stored")]
        v_stored, y_stored = sem("v_stored"), sem("y_stored")
        UNITS = 2 * CT + 2 * JT

        def pairs(eng, body, ahead):
            with eng.Fori(0, BLOCKS // 2 - 1) as i:
                for par in range(2):
                    body(i * 2 + par, par, True)
            for par in range(2):
                body(BLOCKS - 2 + par, par, par == 0 or not ahead)

        block = own.enter_context(nc.Block())

        @block.sync
        def _(sp):
            tokens = lambda t, n: t[bass.ds(n * BLK, BLK), :].rearrange("(j p) c -> p j c", p=P)
            channels = lambda t, n: t[bass.ds((n // TB) * DIM, DIM), bass.ds((n % TB) * BLK, BLK)].rearrange(
                "(g p) t -> p g t", p=P)
            sp.sem_inc(x_loaded[0], PRIME)
            sp.sem_inc(x_loaded[1], PRIME)
            for s in (*qk_stored, v_stored, y_stored):
                sp.sem_inc(s, PRIME)
            for n in range(2):
                sp.dma_start(x_in[:, n], tokens(x, n)).then_inc(x_loaded[n], DMA)

            def body(n, par, ahead):
                for t, names in enumerate((("q_hi", "q_lo"), ("k_hi", "k_lo"))):
                    sp.wait_ge(proj_free, PRIME + n * UNITS + CT * (t + 1))
                    sp.dma_start(channels(dram[names[0]], n), qk_hi[:, t].bitcast(F32)).then_inc(qk_stored[t], DMA)
                    sp.dma_start(channels(dram[names[1]], n), qk_lo[:, t].bitcast(F32)).then_inc(qk_stored[t], DMA)
                sp.wait_ge(proj_free, PRIME + n * UNITS + 2 * CT + JT)
                sp.dma_start(tokens(dram["v"], n), v_out[:]).then_inc(v_stored, DMA)
                sp.wait_ge(y_ready, n * JT + JT)
                sp.dma_start(tokens(dram["y"], n), y_out[:]).then_inc(y_stored, DMA)
                if ahead:
                    sp.dma_start(x_in[:, par], tokens(x, n + 2)).then_inc(x_loaded[par], DMA)

            with sp.Fori(0, BLOCKS // 2 - 1) as i:
                for par in range(2):
                    body(i * 2 + par, par, True)
            for par in range(2):
                body(BLOCKS - 2 + par, par, False)
            for s in qk_stored:
                sp.wait_ge(s, PRIME + 2 * DMA * BLOCKS)
            sp.wait_ge(v_stored, PRIME + DMA * BLOCKS)
            sp.wait_ge(y_stored, PRIME + DMA * BLOCKS)

        @block.gpsimd
        def _(pool):
            def deviation(n, par):
                pool.wait_ge(var_ready, n + 1)
                nc.gpsimd.tensor_tensor(rstd[:], rstd[:], keep["power"][:], ALU.pow).then_inc(rstd_ready, 1)

            def body(n, par, ahead):
                if ahead:
                    deviation(n + 1, 1 - par)
                for j in range(JT):
                    pool.wait_ge(tanh_ready, n * JT + j + 1)
                    nc.gpsimd.tensor_tensor(y_out[:, j], y_out[:, j], x_in[:, par, j], ALU.add).then_inc(half_y, 1)
                    pool.wait_ge(half_y, n * JT + j + 1)
                    nc.gpsimd.tensor_tensor(y_out[:, j], y_out[:, j], keep["row_bias"][:, 2], ALU.add).then_inc(y_ready, 1)

            deviation(0, 0)
            pairs(pool, body, True)

        @block.scalar
        def _(act):
            act.sem_inc(hi_ready, PRIME)

            def turn_high(n, par):
                for c in range(CT):
                    act.wait_ge(turned_ready, n * CT + c + 1)
                    nc.scalar.activation(xt_hi[:, par, c], turned[:, c], ACT.Copy).then_inc(xt_hi_ready, 1)

            def body(n, par, ahead):
                for t in range(2):
                    act.wait_ge(qk_stored[t], PRIME + n * (2 * DMA))
                    for g in range(CT):
                        u = t * CT + g
                        act.wait_ge(proj_ready, n * UNITS + u + 1)
                        nc.scalar.activation(qk_hi[:, t, g], proj[:, u % RING], ACT.Identity,
                                             bias=keep["qk_bias"][:, t, g:g + 1]).then_inc(hi_ready, 1)
                if ahead:
                    turn_high(n + 1, 1 - par)
                for j in range(JT):
                    act.wait_ge(proj_free, PRIME + n * UNITS + 2 * CT + JT + j + 1)
                    nc.scalar.activation(y_out[:, j], y_out[:, j], ACT.Tanh).then_inc(tanh_ready, 1)

            turn_high(0, 0)
            pairs(act, body, True)

        @block.vector
        def _(dve):
            dve.sem_inc(proj_free, PRIME)
            dve.sem_inc(xn_ready, PRIME)

            def moments(n, par):
                dve.wait_ge(x_loaded[par], PRIME + DMA * (n // 2 + 1))
                for j in range(JT):
                    last = nc.vector.bn_stats(stats[:, j], x_in[:, par, j])
                last.then_inc(stats_ready, 1)

            def aggregate(n):
                for j in range(JT):
                    last = nc.vector.bn_aggr(mean_var[:, j], stats[:, j])
                last.then_inc(mean_ready, 1)
                dve.wait_ge(mean_ready, n + 1)
                nc.vector.tensor_scalar(rstd[:], mean_var[:, :, 1], EPS, None, ALU.add).then_inc(var_ready, 1)

            def normalize(n, par):
                dve.wait_ge(rstd_ready, n + 1)
                for j in range(JT):
                    last = nc.vector.tensor_scalar(xn[:, j], x_in[:, par, j], mean_var[:, j, 0:1], rstd[:, j:j + 1],
                                                   ALU.subtract, ALU.mult)
                last.then_inc(xn_ready, 1)

            def turn_low(n, par):
                for c in range(CT):
                    dve.wait_ge(xt_hi_ready, n * CT + c + 1)
                    nc.vector.tensor_tensor(xt_lo[:, par, c], turned[:, c], xt_hi[:, par, c].bitcast(F32),
                                            ALU.subtract).then_inc(xt_lo_ready, 1)

            def body(n, par, ahead):
                if ahead:
                    moments(n + 1, 1 - par)
                for t in range(2):
                    for g in range(CT):
                        u = t * CT + g
                        if u == 0 and ahead:
                            dve.wait_ge(stats_ready, n + 2)
                        dve.wait_ge(hi_ready, PRIME + n * (2 * CT) + u + 1)
                        nc.vector.scalar_tensor_tensor(qk_lo[:, t, g], proj[:, u % RING], keep["qk_bias"][:, t, g:g + 1],
                                                       qk_hi[:, t, g].bitcast(F32), ALU.add,
                                                       ALU.subtract).then_inc(proj_free, 1)
                        if u == 0 and ahead:
                            aggregate(n + 1)
                    if t == 0 and ahead:
                        normalize(n + 1, 1 - par)
                if ahead:
                    turn_low(n + 1, 1 - par)
                for j in range(JT):
                    if j == 0:
                        dve.wait_ge(v_stored, PRIME + n * DMA)
                    u = 2 * CT + j
                    dve.wait_ge(proj_ready, n * UNITS + u + 1)
                    nc.vector.tensor_tensor(v_out[:, j], proj[:, u % RING], keep["row_bias"][:, 0],
                                            ALU.add).then_inc(proj_free, 1)
                for j in range(JT):
                    if j == 0:
                        dve.wait_ge(y_stored, PRIME + n * DMA)
                    u = 2 * CT + JT + j
                    dve.wait_ge(proj_ready, n * UNITS + u + 1)
                    nc.vector.tensor_tensor(y_out[:, j], proj[:, u % RING], keep["row_bias"][:, 1],
                                            ALU.add).then_inc(proj_free, 1)

            moments(0, 0)
            dve.wait_ge(stats_ready, 1)
            aggregate(0)
            normalize(0, 0)
            turn_low(0, 0)
            pairs(dve, body, True)

        @block.tensor
        def _(pe):
            w_hi, w_lo = keep["w_hi"], keep["w_lo"]

            def turn(n, par):
                pe.wait_ge(xn_ready, PRIME + n + 1)
                for c in range(CT):
                    for j in range(JT):
                        last = nc.tensor.transpose(turned[:, c, j * P:(j + 1) * P], xn[:, j, c * P:(c + 1) * P],
                                                   keep["ident"][:])
                    last.then_inc(turned_ready, 1)

            def body(n, par, ahead):
                pe.wait_ge(xt_lo_ready, n * CT + CT)
                x_hi = lambda c: xt_hi[:, par, c]
                x_lo = lambda c: xt_lo[:, par, c]
                for u in range(2 * CT):
                    t, g = divmod(u, CT)
                    pe.wait_ge(proj_free, PRIME + n * UNITS + u - RING + 1)
                    three_passes(nc, proj[:, u % RING], lambda c: w_hi[:, t, c, g * P:(g + 1) * P],
                                 lambda c: w_lo[:, t, c, g * P:(g + 1) * P], x_hi, x_lo).then_inc(proj_ready, 1)
                if ahead:
                    turn(n + 1, 1 - par)
                for u in range(2 * CT, UNITS):
                    t, j = divmod(u - 2 * CT, JT)
                    pe.wait_ge(proj_free, PRIME + n * UNITS + u - RING + 1)
                    three_passes(nc, proj[:, u % RING], lambda c: x_hi(c)[:, j * P:(j + 1) * P],
                                 lambda c: x_lo(c)[:, j * P:(j + 1) * P], lambda c: w_hi[:, 2 + t, c],
                                 lambda c: w_lo[:, 2 + t, c]).then_inc(proj_ready, 1)

            turn(0, 0)
            pairs(pe, body, True)


def build_attend(nc, dram):
    with ExitStack() as own:
        sb = lambda name, shape, dt=F32: own.enter_context(nc.sbuf_tensor(name, shape, dt))
        ps = lambda name, shape: own.enter_context(nc.psum_tensor(name, shape, F32))
        sem = lambda name: own.enter_context(nc.semaphore(name))
        q_st = [sb(f"q_stack{r}", [P, SEQ], F32R) for r in range(GROUP)]
        k_st = [sb(f"k_stack{r}", [P, SEQ], F32R) for r in range(GROUP)]
        v_sb = [sb(f"v_head{r}", [P, KT, DH]) for r in range(GROUP)]
        probs = [sb(f"probs{s}", [P, SEQ]) for s in range(PROBS)]
        pool_sum = [sb(f"pool_sum{s}", [P, SEQ]) for s in range(2)]
        ones, ident = sb("ones_att", [P, DH]), sb("ident_att", [P, P])
        part_max, row_max = sb("part_max", [P, UNITS]), sb("row_max", [P, QT])
        max_row = sb("max_row", [QT, P], F32R)
        pv_copy, sum_copy, recip = sb("pv_copy", [P, BLK]), sb("sum_copy", [P, BLK]), sb("recip", [P, BLK])
        ctx_out = [sb(f"ctx_out{s}", [P, BLK]) for s in range(2)]
        st_bank = ps("st_bank", [P, ST_BANKS, BLK])
        sm_bank = ps("sm_bank", [P, SM_BANKS, BLK])
        pv_bank = ps("pv_bank", [P, BLK])
        sum_bank = ps("sum_bank", [P, BLK])
        consts_ready, ident_zero = sem("consts_ready"), sem("ident_zero")
        head_loaded = [sem(f"head_loaded{r}") for r in range(GROUP)]
        row_loaded = [sem(f"row_loaded{r}") for r in range(GROUP)]
        scores_ready, probs_ready, tile_used = sem("scores_ready"), sem("probs_ready"), sem("tile_used")
        max_scores_ready, max_scores_read = sem("max_scores_ready"), sem("max_scores_read")
        row_max_ready, turned_ready, max_row_ready = sem("row_max_ready"), sem("max_turned"), sem("max_row_ready")
        pool_added, sums_ready, recip_ready, context_ready = sem("pool_added"), sem("sums_ready"), sem("recip_ready"), sem("context_ready")
        banks_copied = sem("banks_copied")
        context_stored = [sem("context_stored0"), sem("context_stored1")]
        HEAD_DMAS = 7
        CTX_DMAS = QB

        def heads(eng, body):
            with eng.Fori(0, ALL_HEADS // GROUP - 1) as i:
                after = eng.snap(i + 1)
                for r in range(GROUP):
                    body(i * GROUP + r, r, 2, after * GROUP + (r + 1 - GROUP))
            for r in range(GROUP):
                body(ALL_HEADS - GROUP + r, r, min(2, GROUP - 1 - r), ALL_HEADS - GROUP + r + 1)

        units_before = [sum(PLAN[:kt]) for kt in range(KT)]

        def read_before(u):
            return u - 2 if u else 0

        assert ST_BANKS == SM_BANKS == 3

        block = own.enter_context(nc.Block())

        @block.sync
        def _(sp):
            for s in (*head_loaded, *row_loaded, *context_stored):
                sp.sem_inc(s, PRIME)

            def load(h, r):
                rows = lambda t: dram[t][bass.ds(h * DH, DH), :]
                for i, t in enumerate(("q_hi", "q_lo", "q_hi")):
                    sp.dma_start(q_st[r][i * DH:(i + 1) * DH, :].bitcast(F32), rows(t)).then_inc(head_loaded[r], DMA)
                for i, t in enumerate(("k_hi", "k_hi", "k_lo")):
                    sp.dma_start(k_st[r][i * DH:(i + 1) * DH, :].bitcast(F32), rows(t)).then_inc(head_loaded[r], DMA)
                v_rows = dram["v"][bass.ds((h // HEADS) * SEQ, SEQ), bass.ds((h % HEADS) * DH, DH)]
                sp.dma_start(v_sb[r][:], v_rows.rearrange("(t p) d -> p t d", p=P)).then_inc(head_loaded[r], DMA)

            def load_row(h, r):
                sp.wait_ge(max_row_ready, h + 1)
                sp.dma_start(q_st[r][MROW:MROW + 1, :].bitcast(F32), max_row[:].bitcast(F32)).then_inc(row_loaded[r], DMA)

            def store(h, r):
                sp.wait_ge(context_ready, PRIME + h + 1)
                for q in range(QB):
                    sp.dma_start(dram["ctx"][bass.ds(h * DH, DH), q * BLK:(q + 1) * BLK],
                                 ctx_out[r % 2][q * DH:(q + 1) * DH, :]).then_inc(context_stored[r % 2], DMA)

            for h in range(GROUP):
                load(h, h)
            load_row(0, 0)
            load_row(1, 1)

            def body(h, r, more, following):
                if more >= 2:
                    load_row(h + 2, (r + 2) % GROUP)
                store(h, r)
                if not isinstance(h, int):
                    load(h + GROUP, r)

            heads(sp, body)
            for s in context_stored:
                sp.wait_ge(s, PRIME + CTX_DMAS * DMA * ALL_HEADS // 2)

        @block.gpsimd
        def _(pool):
            pool.sem_inc(pool_added, PRIME)
            nc.gpsimd.memset(ident[:], 0.0).then_inc(ident_zero, 1)
            nc.gpsimd.memset(ones[:], 1.0).then_inc(consts_ready, 1)
            pool.wait_ge(ident_zero, 1)
            nc.gpsimd.affine_select(out=ident[:], in_=ident[:], compare_op=ALU.not_equal, fill=1.0, base=0,
                                    pattern=[[-1, P]], channel_multiplier=1).then_inc(consts_ready, 1)

            def body(h, r, more, following):
                total = pool_sum[r % 2]
                for i, kt in enumerate(POOL_TILES[1:]):
                    if i == 0:
                        pool.wait_ge(sums_ready, PRIME + h - 1)
                    pool.wait_ge(probs_ready, PRIME + h * (KT * QB) + QB * (kt + 1))
                    if i == 0:
                        one = probs[POOL_TILES[0] % PROBS]
                    else:
                        pool.wait_ge(pool_added, PRIME + h * POOL_ADDS + i)
                        one = total
                    nc.gpsimd.tensor_tensor(total[:], one[:], probs[kt % PROBS][:], ALU.add).then_inc(pool_added, 1)

            heads(pool, body)

        @block.scalar
        def _(act):
            act.sem_inc(probs_ready, PRIME)

            def exps(h, kt):
                for q in range(QB):
                    if q == 0:
                        act.wait_ge(tile_used, PRIME + h * KT + kt - PROBS + 1)
                        old, back = ((kt - PROBS), 0) if kt >= PROBS else (kt - PROBS + KT, 1)
                        if old in POOL_TILES:
                            act.wait_ge(pool_added, PRIME + h * POOL_ADDS - back * POOL_ADDS + adds_after(old))
                    act.wait_ge(scores_ready, h * (KT * QB) + kt * QB + q + 1)
                    nc.scalar.activation(probs[kt % PROBS][:, q * BLK:(q + 1) * BLK],
                                         st_bank[:, (kt * QB + q) % ST_BANKS], ACT.Exp,
                                         scale=SCALE).then_inc(probs_ready, 1)

            def copy_banks(h):
                act.wait_ge(sums_ready, PRIME + h + 1)
                act.wait_ge(context_ready, PRIME + h)
                nc.scalar.activation(pv_copy[:], pv_bank[:], ACT.Copy).then_inc(banks_copied, 1)
                nc.scalar.activation(sum_copy[:], sum_bank[:], ACT.Copy).then_inc(banks_copied, 1)

            exps(0, 0)

            def body(h, r, more, following):
                for kt in range(1, KT):
                    exps(h, kt)
                if more:
                    exps(h + 1, 0)
                copy_banks(h)

            act.sem_inc(banks_copied, PRIME)
            heads(act, body)

        @block.vector
        def _(dve):
            dve.sem_inc(max_scores_read, PRIME)
            dve.sem_inc(context_ready, PRIME)
            dve.sem_inc(row_max_ready, PRIME)
            for r in range(GROUP):
                nc.vector.memset(k_st[r][MROW:MROW + 1, :].bitcast(F32), 1.0).then_inc(consts_ready, 1)

            def maxima(s):
                for k in range(UNITS):
                    if k == 0:
                        dve.wait_ge(row_max_ready, PRIME + s)
                    dve.wait_ge(max_scores_ready, s * UNITS + k + 1)
                    nc.vector.tensor_reduce(part_max[:, k:k + 1], sm_bank[:, k % SM_BANKS], AX.X,
                                            ALU.max).then_inc(max_scores_read, 1)
                dve.wait_ge(max_scores_read, PRIME + s * UNITS + UNITS)
                nc.vector.tensor_reduce(row_max[:], part_max[:].rearrange("p (q b) -> p q b", b=QB), AX.X,
                                        ALU.max).then_inc(row_max_ready, 1)
                dve.wait_ge(turned_ready, s + 1)
                nc.vector.tensor_scalar(max_row[:], sm_bank[0:QT, 0, 0:P], -1.0, None,
                                        ALU.mult).then_inc(max_row_ready, 1)

            def context(h, r):
                dve.wait_ge(banks_copied, PRIME + 2 * h + 2)
                nc.vector.reciprocal(recip[:], sum_copy[:]).then_inc(recip_ready, 1)
                dve.wait_ge(recip_ready, h + 1)
                dve.wait_ge(context_stored[r % 2], PRIME + (h // 2) * (CTX_DMAS * DMA))
                nc.vector.tensor_tensor(ctx_out[r % 2][:], pv_copy[:], recip[:], ALU.mult).then_inc(context_ready, 1)

            maxima(0)
            maxima(1)

            def body(h, r, more, following):
                if more >= 2:
                    maxima(h + 2)
                context(h, r)

            heads(dve, body)

        @block.tensor
        def _(pe):
            pe.sem_inc(tile_used, PRIME)
            pe.sem_inc(sums_ready, PRIME)
            pe.wait_ge(consts_ready, 2 + GROUP)

            def max_scores(s, r, k):
                q, b = divmod(k, QB)
                if k == 0:
                    pe.wait_ge(head_loaded[r], PRIME + (s // GROUP) * (HEAD_DMAS * DMA) + HEAD_DMAS * DMA)
                    if not (isinstance(s, int) and s == 0):
                        pe.wait_ge(max_row_ready, s)
                pe.wait_ge(max_scores_read, PRIME + s * UNITS + read_before(k))
                nc.tensor.matmul(sm_bank[:, k % SM_BANKS], q_st[r][0:ROWS, q * P:(q + 1) * P],
                                 k_st[r][0:ROWS, b * BLK:(b + 1) * BLK], start=True,
                                 stop=True).then_inc(max_scores_ready, 1)

            def scores(h, r, kt, q):
                u = kt * QB + q
                if u == 0:
                    pe.wait_ge(row_loaded[r], PRIME + (h // GROUP) * DMA + DMA)
                pe.wait_ge(probs_ready, PRIME + h * UNITS + read_before(u))
                nc.tensor.matmul(st_bank[:, u % ST_BANKS], k_st[r][0:ROWS + 1, kt * P:(kt + 1) * P],
                                 q_st[r][0:ROWS + 1, q * BLK:(q + 1) * BLK], start=True,
                                 stop=True).then_inc(scores_ready, 1)

            def spread(bank, left, right, start, stop):
                for q in range(QB):
                    last = nc.tensor.matmul(bank[q * DH:(q + 1) * DH, :], left, right[:, q * BLK:(q + 1) * BLK],
                                            start=start, stop=stop)
                return last

            def use(h, r, kt):
                if kt == 0:
                    pe.wait_ge(banks_copied, PRIME + 2 * h)
                pe.wait_ge(probs_ready, PRIME + h * (KT * QB) + QB * (kt + 1))
                tile = probs[kt % PROBS]
                last = spread(pv_bank, v_sb[r][:, kt], tile, kt == 0, kt == KT - 1)
                if kt not in POOL_TILES:
                    first = all(t in POOL_TILES for t in range(kt))
                    last = spread(sum_bank, ones[:], tile, first, False)
                last.then_inc(tile_used, 1)
                if kt == KT - 1:
                    pe.wait_ge(pool_added, PRIME + h * POOL_ADDS + POOL_ADDS)
                    spread(sum_bank, ones[:], pool_sum[r % 2], False, True).then_inc(sums_ready, 1)

            def step(h, r, kt, ahead, last):
                units = list(range(units_before[kt], units_before[kt] + PLAN[kt])) if ahead is not None else []
                r1 = (r + 1) % GROUP
                for q in range(QB):
                    if units:
                        max_scores(ahead, r1, units.pop(0))
                    elif q == ST_BANKS and last:
                        use(*last)
                        last = None
                    scores(h, r, kt, q)
                for k in units:
                    max_scores(ahead, r1, k)
                if last:
                    use(*last)

            def turn_max(s):
                pe.wait_ge(row_max_ready, PRIME + s + 1)
                nc.tensor.transpose(sm_bank[0:QT, 0, 0:P], row_max[:], ident[:]).then_inc(turned_ready, 1)

            for k in range(UNITS):
                max_scores(0, 0, k)
            turn_max(0)
            step(0, 0, 0, 1, None)

            def body(h, r, more, following):
                for kt in range(1, KT):
                    step(h, r, kt, following if more >= 1 else None, (h, r, kt - 1))
                    if kt == MAX_KT and more >= 1:
                        turn_max(h + 1)
                if more >= 1:
                    step(h + 1, (r + 1) % GROUP, 0, following + 1 if more >= 2 else None, (h, r, KT - 1))
                else:
                    use(h, r, KT - 1)

            heads(pe, body)


def build_output(nc, dram, out):
    with ExitStack() as own:
        sb = lambda name, shape, dt=F32: own.enter_context(nc.sbuf_tensor(name, shape, dt))
        sem = lambda name: own.enter_context(nc.semaphore(name))
        wo_hi, wo_lo = sb("wo_hi_sb", [P, CT, DIM], F32R), sb("wo_lo_sb", [P, CT, DIM], F32R)
        ctx_in = [sb(f"ctx_in{s}", [P, CT, BLK]) for s in range(2)]
        y_in = [sb(f"y_in{s}", [P, JT, DIM]) for s in range(2)]
        ctx_hi = [sb(f"ctx_hi{s}", [P, CT, BLK], F32R) for s in range(2)]
        ctx_lo = [sb(f"ctx_lo{s}", [P, CT, BLK], F32R) for s in range(2)]
        res = [sb(f"res{s}", [P, JT, DIM]) for s in range(2)]
        RING = 8
        bank = own.enter_context(nc.psum_tensor("out_bank", [P, RING, BLK], F32))
        w_loaded = sem("wo_loaded")
        ctx_loaded, y_loaded = [sem("ctx_loaded0"), sem("ctx_loaded1")], [sem("y_loaded0"), sem("y_loaded1")]
        hi_ready, lo_ready, bank_ready, res_ready = sem("ctx_hi_ready"), sem("ctx_lo_ready"), sem("out_bank_ready"), sem("res_ready")
        stored = [sem("stored0"), sem("stored1")]

        def pairs(eng, body):
            with eng.Fori(0, BLOCKS // 2 - 1) as i:
                for par in range(2):
                    body(i * 2 + par, par, True)
            for par in range(2):
                body(BLOCKS - 2 + par, par, False)

        block = own.enter_context(nc.Block())
        tokens = lambda t, n: t[bass.ds(n * BLK, BLK), :].rearrange("(j p) c -> p j c", p=P)

        @block.sync
        def _(sp):
            sp.dma_start(wo_hi[:].bitcast(F32), dram["wo_hi"].rearrange("(r p) c -> p r c", p=P)).then_inc(w_loaded, DMA)
            sp.dma_start(wo_lo[:].bitcast(F32), dram["wo_lo"].rearrange("(r p) c -> p r c", p=P)).then_inc(w_loaded, DMA)
            for s in stored:
                sp.sem_inc(s, PRIME)

            def load(n, par):
                src = dram["ctx"][bass.ds((n // TB) * DIM, DIM), bass.ds((n % TB) * BLK, BLK)]
                sp.dma_start(ctx_in[par][:], src.rearrange("(c p) t -> p c t", p=P)).then_inc(ctx_loaded[par], DMA)

            def load_y(n, par):
                sp.dma_start(y_in[par][:], tokens(dram["y"], n)).then_inc(y_loaded[par], DMA)

            for n in range(2):
                load(n, n)
            for n in range(2):
                load_y(n, n)

            def body(n, par, ahead):
                if ahead:
                    sp.wait_ge(lo_ready, n + 1)
                    load(n + 2, par)
                sp.wait_ge(res_ready, PRIME + n * JT + JT)
                sp.dma_start(tokens(out, n), res[par][:]).then_inc(stored[par], DMA)
                if ahead:
                    load_y(n + 2, par)

            pairs(sp, body)
            for s in stored:
                sp.wait_ge(s, PRIME + DMA * BLOCKS // 2)

        @block.scalar
        def _(act):
            act.wait_ge(w_loaded, 2 * DMA)

            def body(n, par, ahead):
                act.wait_ge(ctx_loaded[par], (n // 2) * DMA + DMA)
                act.wait_ge(res_ready, PRIME + n * JT - JT)
                nc.scalar.activation(ctx_hi[par][:], ctx_in[par][:], ACT.Copy).then_inc(hi_ready, 1)

            pairs(act, body)

        @block.vector
        def _(dve):
            dve.sem_inc(res_ready, PRIME)

            def low(n, par):
                dve.wait_ge(hi_ready, n + 1)
                nc.vector.tensor_tensor(ctx_lo[par][:], ctx_in[par][:], ctx_hi[par][:].bitcast(F32),
                                        ALU.subtract).then_inc(lo_ready, 1)

            low(0, 0)

            def body(n, par, ahead):
                if ahead or par == 0:
                    low(n + 1, 1 - par)
                dve.wait_ge(y_loaded[par], (n // 2) * DMA + DMA)
                dve.wait_ge(stored[par], PRIME + (n // 2) * DMA)
                for j in range(JT):
                    dve.wait_ge(bank_ready, n * JT + j + 1)
                    nc.vector.tensor_tensor(res[par][:, j], bank[:, JT * par + j], y_in[par][:, j],
                                            ALU.add).then_inc(res_ready, 1)

            pairs(dve, body)

        @block.tensor
        def _(pe):
            pe.wait_ge(w_loaded, 2 * DMA)

            def body(n, par, ahead):
                pe.wait_ge(lo_ready, n + 1)
                for j in range(JT):
                    pe.wait_ge(res_ready, PRIME + n * JT + j - RING + 1)
                    three_passes(nc, bank[:, JT * par + j], lambda c: ctx_hi[par][:, c, j * P:(j + 1) * P],
                                 lambda c: ctx_lo[par][:, c, j * P:(j + 1) * P], lambda c: wo_hi[:, c],
                                 lambda c: wo_lo[:, c]).then_inc(bank_ready, 1)

            pairs(pe, body)


def build_program(nc, x, w, out):
    x, out = x.flatten_outer_dims(), out.flatten_outer_dims()
    scratch = lambda name, shape: nc.dram_tensor(name, shape, F32, kind="Internal").ap()
    dram = {n: scratch(f"s_{n}", [BATCH * DIM, SEQ]) for n in ("q_hi", "q_lo", "k_hi", "k_lo", "ctx")}
    dram |= {n: scratch(f"s_{n}", [BATCH * SEQ, DIM]) for n in ("v", "y")}
    dram |= {n: scratch(f"s_{n}", [DIM, DIM]) for n in ("wo_hi", "wo_lo")}
    with ExitStack() as ctx:
        sb = lambda name, shape, dt=F32: ctx.enter_context(nc.sbuf_tensor(name, shape, dt))
        keep = {
            "ident": sb("ident", [P, P]), "ones": sb("ones", [P, DH]), "power": sb("power", [P, JT]),
            "qk_bias": sb("qk_bias", [P, 2, CT]), "row_bias": sb("row_bias", [P, 3, DIM]),
            "w_hi": sb("w_hi", [P, 4, CT, DIM], F32R), "w_lo": sb("w_lo", [P, 4, CT, DIM], F32R),
        }
        build_weights(nc, ctx, w, dram, keep)
        build_project(nc, x, dram, keep)
    build_attend(nc, dram)
    build_output(nc, dram, out)


_NAMES = {
    "x": "L0_attn_query", "q": "L0_attn_q_w", "q_b": "L0_attn_q_b", "k": "L0_attn_k_w", "k_b": "L0_attn_k_b",
    "v": "L0_attn_v_w", "v_b": "L0_attn_v_b", "o": "L0_attn_out_w", "o_b": "L0_attn_out_b",
    "w": "L0_ffn_weight", "a1": "L0_ffn_aux_weight1", "a2": "L0_ffn_aux_weight2", "ffn_b": "L0_ffn_bias",
}


def kernel(**inputs):
    import numpy as np
    import concourse.bacc as bacc
    from concourse.bass_utils import run_bass_kernel_spmd

    nc = bacc.Bacc("TRN2", target_bir_lowering=False, num_devices=1)
    arrays, given = {}, {}
    for short, name in _NAMES.items():
        a = np.ascontiguousarray(inputs[name])
        arrays[f"in_{short}"] = a
        given[short] = nc.dram_tensor(f"in_{short}", a.shape, mybir.dt.from_np(a.dtype), kind="ExternalInput").ap()
    x = given.pop("x")
    out = nc.dram_tensor("out_0", x.shape, F32, kind="ExternalOutput").ap()
    build_program(nc, x, given, out)
    r = run_bass_kernel_spmd(nc, [arrays], core_ids=[0])
    return r.results[0]["out_0"]
```

```python
from contextlib import ExitStack

import concourse.bass as bass
from concourse import mybir

F32 = mybir.dt.float32
F32R = mybir.dt.float32r
ACT = mybir.ActivationFunctionType
ALU = mybir.AluOpType
AX = mybir.AxisListType

P = 128
BATCH, SEQ, DIM = 4, 2048, 512
HEADS = 16
DH = DIM // HEADS
CT = DIM // P
BLK = 512
JT = BLK // P
BLOCKS = BATCH * SEQ // BLK
TB = SEQ // BLK
EPS = 1e-5
SCALE = float(DH) ** -0.5
DMA = 16
PRIME = 16

KT = SEQ // P
QT = SEQ // P
QB = SEQ // BLK
ALL_HEADS = BATCH * HEADS
GROUP = 4
ROWS = 3 * DH
MROW = ROWS
PROBS = 8
ST_BANKS = 3
SM_BANKS = 3
UNITS = KT * QB
PER_TILE = UNITS // KT
AHEAD = 3
TURN_UNIT = PER_TILE
POOL_TILES = list(range(11))
DVE_TILES = [11, 12, 13]
POOL_SUM_KT, DVE_SUM_KT = 2, 5
CUT = 6
POOL_ADDS = len(POOL_TILES) - 1
DVE_CHUNKS = QB * (len(DVE_TILES) - 1)
PACK = SEQ // P
SUM_WORK = {8: 0, 10: 1, 12: 2, 14: 3, 20: 4, 22: 5, 24: 6, 28: 7}
RECIP_UNIT, SCALE_UNIT = 16, 34


def place(u):
    return u % 3 if u < UNITS // 2 else (UNITS - 2 - u) % 3


def read_before(u):
    return next(v for v in range(u - 1, u - UNITS, -1) if place(v % UNITS) == place(u)) + 1


assert UNITS == 64 and ST_BANKS == SM_BANKS == 3
assert min(u + 1 - read_before(u) for u in range(UNITS)) == 2


def adds_after(kt):
    return max(1, POOL_TILES.index(kt))


def chunks_after(kt):
    return QB * max(1, DVE_TILES.index(kt))


def build_weights(nc, ctx, w, dram, keep):
    with ExitStack() as own:
        sb = lambda name, shape, dt=F32: own.enter_context(nc.sbuf_tensor(name, shape, dt))
        sem = lambda name: own.enter_context(nc.semaphore(name))
        raw = {n: sb(f"raw_{n}", [P, CT, DIM]) for n in ("a1", "w", "a2", "q", "k", "v", "o")}
        a1_t, w_t, m1 = sb("a1_t", [P, CT, DIM]), sb("w_t", [P, CT, DIM]), sb("m1", [P, CT, DIM])
        o_hi, o_lo = sb("o_hi", [P, CT, DIM], F32R), sb("o_lo", [P, CT, DIM], F32R)
        bank = own.enter_context(nc.psum_tensor("w_bank", [P, 8, BLK], F32))
        loaded = {n: sem(f"loaded_{n}") for n in raw}
        ident_ready, bank_ready, high_ready, bank_free = sem("ident_ready"), sem("bank_ready"), sem("high_ready"), sem("bank_free")
        small_loaded, wo_stored = sem("small_loaded"), sem("wo_stored")

        split = {"q": 0, "k": 1, "v": 2}
        banks = [("turn", n, c) for n in ("a1", "w") for c in range(CT)]
        banks += [("m1", "m1", c) for c in range(CT)]
        banks += [("turn", n, c) for n in ("q", "k", "v", "o") for c in range(CT)]
        banks += [("ffn", "ffn", c) for c in range(CT)]
        plain = {"a1": a1_t, "w": w_t, "m1": m1}
        high = lambda n: o_hi if n == "o" else keep["w_hi"][:, split.get(n, 3)]
        low = lambda n: o_lo if n == "o" else keep["w_lo"][:, split.get(n, 3)]
        first_m1 = 2 * CT
        splits = [i for i, (_, n, _) in enumerate(banks) if n not in plain]

        block = own.enter_context(nc.Block())

        @block.sync
        def _(sp):
            for n in ("a1", "w", "a2", "q", "k", "v", "o"):
                sp.dma_start(raw[n][:], w[n].rearrange("(r p) c -> p r c", p=P)).then_inc(loaded[n], DMA)
            sp.wait_ge(bank_free, 2 * CT + CT + 4 * CT)
            sp.dma_start(dram["wo_hi"].rearrange("(r p) c -> p r c", p=P), o_hi[:].bitcast(F32)).then_inc(wo_stored, DMA)
            sp.dma_start(dram["wo_lo"].rearrange("(r p) c -> p r c", p=P), o_lo[:].bitcast(F32)).then_inc(wo_stored, DMA)
            sp.wait_ge(wo_stored, 2 * DMA)

        @block.gpsimd
        def _(pool):
            nc.gpsimd.memset(keep["ident"][:], 0.0).then_inc(ident_ready, 1)
            nc.gpsimd.memset(keep["ones"][:], 1.0)
            nc.gpsimd.memset(keep["power"][:], -0.5)
            pool.wait_ge(ident_ready, 1)
            nc.gpsimd.affine_select(out=keep["ident"][:], in_=keep["ident"][:], compare_op=ALU.not_equal, fill=1.0,
                                    base=0, pattern=[[-1, P]], channel_multiplier=1).then_inc(ident_ready, 1)

        @block.scalar
        def _(act):
            act.dma_start(keep["qk_bias"][:, 0], w["q_b"].rearrange("(g p) -> p g", p=P),
                          allow_slow_non_contiguous=True).then_inc(small_loaded, DMA)
            act.dma_start(keep["qk_bias"][:, 1], w["k_b"].rearrange("(g p) -> p g", p=P),
                          allow_slow_non_contiguous=True).then_inc(small_loaded, DMA)
            for i, n in enumerate(("v_b", "ffn_b", "o_b")):
                act.dma_start(keep["row_bias"][:, i], w[n].partition_broadcast(P)).then_inc(small_loaded, DMA)
            for i in splits:
                act.wait_ge(bank_ready, i + 1)
                _, n, c = banks[i]
                nc.scalar.activation(high(n)[:, c], bank[:, i % 8], ACT.Copy).then_inc(high_ready, 1)
            act.wait_ge(small_loaded, 5 * DMA)

        @block.vector
        def _(dve):
            for i, (_, n, c) in enumerate(banks):
                if n in plain:
                    dve.wait_ge(bank_ready, i + 1)
                    nc.vector.tensor_copy(plain[n][:, c], bank[:, i % 8]).then_inc(bank_free, 1)
                else:
                    dve.wait_ge(high_ready, splits.index(i) + 1)
                    nc.vector.tensor_tensor(low(n)[:, c], bank[:, i % 8], high(n)[:, c].bitcast(F32),
                                            ALU.subtract).then_inc(bank_free, 1)

        @block.tensor
        def _(pe):
            pe.wait_ge(ident_ready, 2)
            for i, (kind, n, c) in enumerate(banks):
                if i >= 8:
                    pe.wait_ge(bank_free, i - 7)
                if kind == "turn":
                    if c == 0:
                        pe.wait_ge(loaded[n], DMA)
                    for r in range(CT):
                        last = nc.tensor.transpose(bank[:, i % 8, r * P:(r + 1) * P], raw[n][:, r, c * P:(c + 1) * P],
                                                   keep["ident"][:])
                else:
                    left, right = (a1_t, raw["a2"]) if kind == "m1" else (w_t, m1)
                    if c == 0:
                        pe.wait_ge(bank_free, first_m1 if kind == "m1" else first_m1 + CT)
                        if kind == "m1":
                            pe.wait_ge(loaded["a2"], DMA)
                    for r in range(CT):
                        last = nc.tensor.matmul(bank[:, i % 8], left[:, r, c * P:(c + 1) * P], right[:, r],
                                                start=(r == 0), stop=(r == CT - 1))
                last.then_inc(bank_ready, 1)


def three_passes(nc, out, left_hi, left_lo, right_hi, right_lo):
    for c in range(CT):
        for n, (a, b) in enumerate(((left_hi, right_hi), (left_hi, right_lo), (left_lo, right_hi))):
            last = nc.tensor.matmul(out, a(c), b(c), start=(c == 0 and n == 0), stop=(c == CT - 1 and n == 2))
    return last


def build_project(nc, x, dram, keep):
    with ExitStack() as own:
        sb = lambda name, shape, dt=F32: own.enter_context(nc.sbuf_tensor(name, shape, dt))
        sem = lambda name: own.enter_context(nc.semaphore(name))
        x_in = sb("x_in", [P, 2, JT, DIM])
        stats, mean_var, rstd = sb("stats", [P, JT, 6]), sb("mean_var", [P, JT, 2]), sb("rstd", [P, JT])
        xn = sb("xn", [P, JT, DIM])
        xt_hi, xt_lo = sb("xt_hi", [P, 2, CT, BLK], F32R), sb("xt_lo", [P, 2, CT, BLK], F32R)
        qk_hi, qk_lo = sb("qk_hi", [P, 2, CT, BLK], F32R), sb("qk_lo", [P, 2, CT, BLK], F32R)
        v_out, y_out = sb("v_out", [P, JT, DIM]), sb("y_out", [P, JT, DIM])
        turned = own.enter_context(nc.psum_tensor("turned", [P, CT, BLK], F32))
        RING = 4
        proj = own.enter_context(nc.psum_tensor("proj", [P, RING, BLK], F32))
        x_loaded = [sem("x_loaded0"), sem("x_loaded1")]
        stats_ready, mean_ready, var_ready, rstd_ready = sem("stats_ready"), sem("mean_ready"), sem("var_ready"), sem("rstd_ready")
        xn_ready, turned_ready, xt_hi_ready, xt_lo_ready = sem("xn_ready"), sem("turned_ready"), sem("xt_hi_ready"), sem("xt_lo_ready")
        proj_ready, hi_ready, proj_free = sem("proj_ready"), sem("hi_ready"), sem("proj_free")
        tanh_ready, half_y, y_ready = sem("tanh_ready"), sem("half_y"), sem("y_ready")
        qk_stored = [sem("q_stored"), sem("k_stored")]
        v_stored, y_stored = sem("v_stored"), sem("y_stored")
        UNITS = 2 * CT + 2 * JT

        def pairs(eng, body, ahead):
            with eng.Fori(0, BLOCKS // 2 - 1) as i:
                for par in range(2):
                    body(i * 2 + par, par, True)
            for par in range(2):
                body(BLOCKS - 2 + par, par, par == 0 or not ahead)

        block = own.enter_context(nc.Block())

        @block.sync
        def _(sp):
            tokens = lambda t, n: t[bass.ds(n * BLK, BLK), :].rearrange("(j p) c -> p j c", p=P)
            channels = lambda t, n: t[bass.ds((n // TB) * DIM, DIM), bass.ds((n % TB) * BLK, BLK)].rearrange(
                "(g p) t -> p g t", p=P)
            sp.sem_inc(x_loaded[0], PRIME)
            sp.sem_inc(x_loaded[1], PRIME)
            for s in (*qk_stored, v_stored, y_stored):
                sp.sem_inc(s, PRIME)
            for n in range(2):
                sp.dma_start(x_in[:, n], tokens(x, n)).then_inc(x_loaded[n], DMA)

            def body(n, par, ahead):
                for t, names in enumerate((("q_hi", "q_lo"), ("k_hi", "k_lo"))):
                    sp.wait_ge(proj_free, PRIME + n * UNITS + CT * (t + 1))
                    sp.dma_start(channels(dram[names[0]], n), qk_hi[:, t].bitcast(F32)).then_inc(qk_stored[t], DMA)
                    sp.dma_start(channels(dram[names[1]], n), qk_lo[:, t].bitcast(F32)).then_inc(qk_stored[t], DMA)
                sp.wait_ge(proj_free, PRIME + n * UNITS + 2 * CT + JT)
                sp.dma_start(tokens(dram["v"], n), v_out[:]).then_inc(v_stored, DMA)
                sp.wait_ge(y_ready, n * JT + JT)
                sp.dma_start(tokens(dram["y"], n), y_out[:]).then_inc(y_stored, DMA)
                if ahead:
                    sp.dma_start(x_in[:, par], tokens(x, n + 2)).then_inc(x_loaded[par], DMA)

            with sp.Fori(0, BLOCKS // 2 - 1) as i:
                for par in range(2):
                    body(i * 2 + par, par, True)
            for par in range(2):
                body(BLOCKS - 2 + par, par, False)
            for s in qk_stored:
                sp.wait_ge(s, PRIME + 2 * DMA * BLOCKS)
            sp.wait_ge(v_stored, PRIME + DMA * BLOCKS)
            sp.wait_ge(y_stored, PRIME + DMA * BLOCKS)

        @block.gpsimd
        def _(pool):
            def deviation(n, par):
                pool.wait_ge(var_ready, n + 1)
                nc.gpsimd.tensor_tensor(rstd[:], rstd[:], keep["power"][:], ALU.pow).then_inc(rstd_ready, 1)

            def body(n, par, ahead):
                if ahead:
                    deviation(n + 1, 1 - par)
                for j in range(JT):
                    pool.wait_ge(tanh_ready, n * JT + j + 1)
                    nc.gpsimd.tensor_tensor(y_out[:, j], y_out[:, j], x_in[:, par, j], ALU.add).then_inc(half_y, 1)
                    pool.wait_ge(half_y, n * JT + j + 1)
                    nc.gpsimd.tensor_tensor(y_out[:, j], y_out[:, j], keep["row_bias"][:, 2], ALU.add).then_inc(y_ready, 1)

            deviation(0, 0)
            pairs(pool, body, True)

        @block.scalar
        def _(act):
            act.sem_inc(hi_ready, PRIME)

            def turn_high(n, par):
                for c in range(CT):
                    act.wait_ge(turned_ready, n * CT + c + 1)
                    nc.scalar.activation(xt_hi[:, par, c], turned[:, c], ACT.Copy).then_inc(xt_hi_ready, 1)

            def body(n, par, ahead):
                for t in range(2):
                    act.wait_ge(qk_stored[t], PRIME + n * (2 * DMA))
                    for g in range(CT):
                        u = t * CT + g
                        act.wait_ge(proj_ready, n * UNITS + u + 1)
                        nc.scalar.activation(qk_hi[:, t, g], proj[:, u % RING], ACT.Identity,
                                             bias=keep["qk_bias"][:, t, g:g + 1]).then_inc(hi_ready, 1)
                if ahead:
                    turn_high(n + 1, 1 - par)
                for j in range(JT):
                    act.wait_ge(proj_free, PRIME + n * UNITS + 2 * CT + JT + j + 1)
                    nc.scalar.activation(y_out[:, j], y_out[:, j], ACT.Tanh).then_inc(tanh_ready, 1)

            turn_high(0, 0)
            pairs(act, body, True)

        @block.vector
        def _(dve):
            dve.sem_inc(proj_free, PRIME)
            dve.sem_inc(xn_ready, PRIME)

            def moments(n, par):
                dve.wait_ge(x_loaded[par], PRIME + DMA * (n // 2 + 1))
                for j in range(JT):
                    last = nc.vector.bn_stats(stats[:, j], x_in[:, par, j])
                last.then_inc(stats_ready, 1)

            def aggregate(n):
                for j in range(JT):
                    last = nc.vector.bn_aggr(mean_var[:, j], stats[:, j])
                last.then_inc(mean_ready, 1)
                dve.wait_ge(mean_ready, n + 1)
                nc.vector.tensor_scalar(rstd[:], mean_var[:, :, 1], EPS, None, ALU.add).then_inc(var_ready, 1)

            def normalize(n, par):
                dve.wait_ge(rstd_ready, n + 1)
                for j in range(JT):
                    last = nc.vector.tensor_scalar(xn[:, j], x_in[:, par, j], mean_var[:, j, 0:1], rstd[:, j:j + 1],
                                                   ALU.subtract, ALU.mult)
                last.then_inc(xn_ready, 1)

            def turn_low(n, par):
                for c in range(CT):
                    dve.wait_ge(xt_hi_ready, n * CT + c + 1)
                    nc.vector.tensor_tensor(xt_lo[:, par, c], turned[:, c], xt_hi[:, par, c].bitcast(F32),
                                            ALU.subtract).then_inc(xt_lo_ready, 1)

            def body(n, par, ahead):
                for u in range(2 * CT):
                    t, g = divmod(u, CT)
                    if u == CT and ahead:
                        moments(n + 1, 1 - par)
                        dve.wait_ge(stats_ready, n + 2)
                    dve.wait_ge(hi_ready, PRIME + n * (2 * CT) + u + 1)
                    nc.vector.scalar_tensor_tensor(qk_lo[:, t, g], proj[:, u % RING], keep["qk_bias"][:, t, g:g + 1],
                                                   qk_hi[:, t, g].bitcast(F32), ALU.add,
                                                   ALU.subtract).then_inc(proj_free, 1)
                    if u == CT and ahead:
                        aggregate(n + 1)
                    if u == CT + 1 and ahead:
                        normalize(n + 1, 1 - par)
                if ahead:
                    turn_low(n + 1, 1 - par)
                for j in range(JT):
                    if j == 0:
                        dve.wait_ge(v_stored, PRIME + n * DMA)
                    u = 2 * CT + j
                    dve.wait_ge(proj_ready, n * UNITS + u + 1)
                    nc.vector.tensor_tensor(v_out[:, j], proj[:, u % RING], keep["row_bias"][:, 0],
                                            ALU.add).then_inc(proj_free, 1)
                for j in range(JT):
                    if j == 0:
                        dve.wait_ge(y_stored, PRIME + n * DMA)
                    u = 2 * CT + JT + j
                    dve.wait_ge(proj_ready, n * UNITS + u + 1)
                    nc.vector.tensor_tensor(y_out[:, j], proj[:, u % RING], keep["row_bias"][:, 1],
                                            ALU.add).then_inc(proj_free, 1)

            moments(0, 0)
            dve.wait_ge(stats_ready, 1)
            aggregate(0)
            normalize(0, 0)
            turn_low(0, 0)
            pairs(dve, body, True)

        @block.tensor
        def _(pe):
            w_hi, w_lo = keep["w_hi"], keep["w_lo"]

            def turn(n, par):
                pe.wait_ge(xn_ready, PRIME + n + 1)
                for c in range(CT):
                    for j in range(JT):
                        last = nc.tensor.transpose(turned[:, c, j * P:(j + 1) * P], xn[:, j, c * P:(c + 1) * P],
                                                   keep["ident"][:])
                    last.then_inc(turned_ready, 1)

            def body(n, par, ahead):
                pe.wait_ge(xt_lo_ready, n * CT + CT)
                x_hi = lambda c: xt_hi[:, par, c]
                x_lo = lambda c: xt_lo[:, par, c]
                for u in range(2 * CT):
                    t, g = divmod(u, CT)
                    pe.wait_ge(proj_free, PRIME + n * UNITS + u - RING + 1)
                    three_passes(nc, proj[:, u % RING], lambda c: w_hi[:, t, c, g * P:(g + 1) * P],
                                 lambda c: w_lo[:, t, c, g * P:(g + 1) * P], x_hi, x_lo).then_inc(proj_ready, 1)
                if ahead:
                    turn(n + 1, 1 - par)
                for u in range(2 * CT, UNITS):
                    t, j = divmod(u - 2 * CT, JT)
                    pe.wait_ge(proj_free, PRIME + n * UNITS + u - RING + 1)
                    three_passes(nc, proj[:, u % RING], lambda c: x_hi(c)[:, j * P:(j + 1) * P],
                                 lambda c: x_lo(c)[:, j * P:(j + 1) * P], lambda c: w_hi[:, 2 + t, c],
                                 lambda c: w_lo[:, 2 + t, c]).then_inc(proj_ready, 1)

            turn(0, 0)
            pairs(pe, body, True)


def build_attend(nc, dram, out):
    with ExitStack() as own:
        sb = lambda name, shape, dt=F32: own.enter_context(nc.sbuf_tensor(name, shape, dt))
        ps = lambda name, shape: own.enter_context(nc.psum_tensor(name, shape, F32))
        sem = lambda name: own.enter_context(nc.semaphore(name))
        q_st = [sb(f"q_stack{r}", [P, SEQ], F32R) for r in range(GROUP)]
        k_st = [sb(f"k_stack{r}", [P, SEQ], F32R) for r in range(GROUP)]
        v_sb = [sb(f"v_head{r}", [P, KT, DH]) for r in range(GROUP)]
        probs = [sb(f"probs{s}", [P, SEQ]) for s in range(PROBS)]
        pool_sum = [sb(f"pool_sum{s}", [P, SEQ]) for s in range(2)]
        dve_sum = sb("dve_sum", [P, SEQ])
        ones, ident = sb("ones_att", [P, DH]), sb("ident_att", [P, P])
        part_max, row_max = sb("part_max", [P, UNITS]), sb("row_max", [P, QT])
        max_row = sb("max_row", [QT, P], F32R)
        pv_copy = [sb(f"pv_copy{s}", [P, BLK]) for s in range(2)]
        sum_copy = [sb(f"sum_copy{s}", [P, BLK]) for s in range(2)]
        sums_col, ratio_col, ratio = sb("sums_col", [P, PACK]), sb("ratio_col", [P, PACK]), sb("ratio", [P, BLK])
        ctx_out = [sb(f"ctx_out{s}", [P, BLK]) for s in range(2)]
        st_bank = ps("st_bank", [P, ST_BANKS, BLK])
        sm_bank = ps("sm_bank", [P, SM_BANKS, BLK])
        pv_bank = ps("pv_bank", [P, BLK])
        sum_bank = ps("sum_bank", [P, BLK])
        consts_ready, ident_zero = sem("consts_ready"), sem("ident_zero")
        head_loaded = [sem(f"head_loaded{r}") for r in range(GROUP)]
        row_loaded = [sem(f"row_loaded{r}") for r in range(GROUP)]
        scores_ready, probs_ready, tile_used = sem("scores_ready"), sem("probs_ready"), sem("tile_used")
        max_scores_ready, max_scores_read = sem("max_scores_ready"), sem("max_scores_read")
        row_max_ready, turned_ready, max_row_ready = sem("row_max_ready"), sem("max_turned"), sem("max_row_ready")
        pool_added, sums_ready, recip_ready, context_ready = sem("pool_added"), sem("sums_ready"), sem("recip_ready"), sem("context_ready")
        pv_copied, sums_copied, dve_added = sem("pv_copied"), sem("sums_copied"), sem("dve_added")
        sums_stored, sums_loaded, ratio_stored, ratio_loaded = sem("sums_stored"), sem("sums_loaded"), sem("ratio_stored"), sem("ratio_loaded")
        context_stored = [sem("context_stored0"), sem("context_stored1")]
        wo_hi, wo_lo = sb("wo_hi_sb", [P, CT, DIM], F32R), sb("wo_lo_sb", [P, CT, DIM], F32R)
        tiled = lambda t: t[:].rearrange("p (c t) -> p c t", c=CT)
        ctx_in = [tiled(q_st[0]).bitcast(F32), tiled(k_st[0]).bitcast(F32)]
        y_in = [tiled(pool_sum[0]), tiled(q_st[3]).bitcast(F32)]
        ctx_hi, ctx_lo = [tiled(q_st[2]), tiled(q_st[1])], [tiled(k_st[2]), tiled(k_st[1])]
        res = [tiled(probs[DVE_TILES[0] % PROBS]), tiled(probs[DVE_TILES[1] % PROBS])]
        out_banks = [sm_bank[:, 0], sm_bank[:, 1], sm_bank[:, 2], st_bank[:, 0]]
        assert len(out_banks) == JT and BLK == DIM
        w_loaded = sem("wo_loaded")
        ctx_loaded, y_loaded = [sem("ctx_loaded0"), sem("ctx_loaded1")], [sem("y_loaded0"), sem("y_loaded1")]
        hi_ready, lo_ready, bank_ready, res_ready = sem("ctx_hi_ready"), sem("ctx_lo_ready"), sem("out_bank_ready"), sem("res_ready")
        stored = [sem("stored0"), sem("stored1")]
        HEAD_DMAS = 7
        CTX_DMAS = QB

        def heads(eng, body):
            with eng.Fori(0, ALL_HEADS // GROUP - 1) as i:
                after = eng.snap(i + 1)
                for r in range(GROUP):
                    body(i * GROUP + r, r, GROUP, after * GROUP + (r + 1 - GROUP))
            for r in range(GROUP):
                body(ALL_HEADS - GROUP + r, r, GROUP - 1 - r, ALL_HEADS - GROUP + r + 1)

        def block_pairs(eng, body):
            with eng.Fori(1, BLOCKS // 2 - 1) as i:
                for par in range(2):
                    body(i * 2 + par, par, True)
            for par in range(2):
                body(BLOCKS - 2 + par, par, False)


        block = own.enter_context(nc.Block())

        @block.sync
        def _(sp):
            for s in (*head_loaded, *row_loaded, *context_stored, *stored):
                sp.sem_inc(s, PRIME)

            def load(h, r):
                rows = lambda t: dram[t][bass.ds(h * DH, DH), :]
                for i, t in enumerate(("q_hi", "q_lo", "q_hi")):
                    sp.dma_start(q_st[r][i * DH:(i + 1) * DH, :].bitcast(F32), rows(t)).then_inc(head_loaded[r], DMA)
                for i, t in enumerate(("k_hi", "k_hi", "k_lo")):
                    sp.dma_start(k_st[r][i * DH:(i + 1) * DH, :].bitcast(F32), rows(t)).then_inc(head_loaded[r], DMA)
                v_rows = dram["v"][bass.ds((h // HEADS) * SEQ, SEQ), bass.ds((h % HEADS) * DH, DH)]
                sp.dma_start(v_sb[r][:], v_rows.rearrange("(t p) d -> p t d", p=P)).then_inc(head_loaded[r], DMA)

            def load_row(h, r):
                sp.wait_ge(max_row_ready, h + 1)
                sp.dma_start(q_st[r][MROW:MROW + 1, :].bitcast(F32), max_row[:].bitcast(F32)).then_inc(row_loaded[r], DMA)

            def spread_ratios(h, r):
                sp.wait_ge(sums_copied, PRIME + h + 1)
                sp.dma_start(dram["sums"][r % 2:r % 2 + 1, :].rearrange("o (q t) -> (o q) t", q=QB),
                             sum_copy[r % 2][0:P:DH, :]).then_inc(sums_stored, DMA)
                sp.wait_ge(sums_stored, h * DMA + DMA)
                sp.dma_start(sums_col[:], dram["sums"][r % 2:r % 2 + 1, :].rearrange("o (p c) -> (o p) c", p=P)
                             ).then_inc(sums_loaded, DMA)
                sp.wait_ge(recip_ready, h + 1)
                sp.dma_start(dram["ratio"][r % 2:r % 2 + 1, :].rearrange("o (p c) -> (o p) c", p=P),
                             ratio_col[:]).then_inc(ratio_stored, DMA)
                sp.wait_ge(ratio_stored, h * DMA + DMA)
                for q in range(QB):
                    row = dram["ratio"][r % 2:r % 2 + 1, q * BLK:(q + 1) * BLK]
                    sp.dma_start(ratio[q * DH:(q + 1) * DH, :], row.broadcast_to([DH, BLK])).then_inc(ratio_loaded, DMA)

            def store(h, r):
                sp.wait_ge(context_ready, PRIME + h + 1)
                for q in range(QB):
                    sp.dma_start(dram["ctx"][bass.ds(h * DH, DH), q * BLK:(q + 1) * BLK],
                                 ctx_out[r % 2][q * DH:(q + 1) * DH, :]).then_inc(context_stored[r % 2], DMA)

            def load_context(n, par):
                src = dram["ctx"][bass.ds((n // TB) * DIM, DIM), bass.ds((n % TB) * BLK, BLK)]
                sp.dma_start(ctx_in[par], src.rearrange("(c p) t -> p c t", p=P)).then_inc(ctx_loaded[par], DMA)

            tokens = lambda t, n: t[bass.ds(n * BLK, BLK), :].rearrange("(j p) c -> p j c", p=P)

            def load_y(n, par):
                sp.dma_start(y_in[par], tokens(dram["y"], n)).then_inc(y_loaded[par], DMA)

            def store_result(n, par):
                sp.wait_ge(res_ready, PRIME + n * JT + JT)
                sp.dma_start(tokens(out, n), res[par]).then_inc(stored[par], DMA)

            for h in range(GROUP):
                load(h, h)
            load_row(0, 0)
            load_row(1, 1)

            def body(h, r, more, following):
                if more >= 2:
                    load_row(following + 1, (r + 2) % GROUP)
                if more == 0:
                    for n in range(2):
                        sp.wait_ge(lo_ready, n + 1)
                        load_context(n + 2, n)
                    load_y(1, 1)
                    store_result(0, 0)
                    load_y(2, 0)
                spread_ratios(h, r)
                store(h, r)
                if not isinstance(h, int):
                    load(h + GROUP, r)
                elif more == 2:
                    sp.dma_start(wo_hi[:].bitcast(F32), dram["wo_hi"].rearrange("(r p) c -> p r c", p=P)).then_inc(w_loaded, DMA)
                    sp.dma_start(wo_lo[:].bitcast(F32), dram["wo_lo"].rearrange("(r p) c -> p r c", p=P)).then_inc(w_loaded, DMA)
                    for n in range(2):
                        load_context(n, n)
                elif more == 1:
                    load_y(0, 0)

            heads(sp, body)
            store_result(1, 1)
            load_y(3, 1)
            for s in context_stored:
                sp.wait_ge(s, PRIME + CTX_DMAS * DMA * ALL_HEADS // 2)

            def output(n, par, ahead):
                if ahead:
                    sp.wait_ge(lo_ready, n + 1)
                    load_context(n + 2, par)
                store_result(n, par)
                if ahead:
                    load_y(n + 2, par)

            block_pairs(sp, output)
            for s in stored:
                sp.wait_ge(s, PRIME + DMA * BLOCKS // 2)

        @block.gpsimd
        def _(pool):
            pool.sem_inc(pool_added, PRIME)
            nc.gpsimd.memset(ident[:], 0.0).then_inc(ident_zero, 1)
            nc.gpsimd.memset(ones[:], 1.0).then_inc(consts_ready, 1)
            pool.wait_ge(ident_zero, 1)
            nc.gpsimd.affine_select(out=ident[:], in_=ident[:], compare_op=ALU.not_equal, fill=1.0, base=0,
                                    pattern=[[-1, P]], channel_multiplier=1).then_inc(consts_ready, 1)

            def body(h, r, more, following):
                total = pool_sum[r % 2]
                for i, kt in enumerate(POOL_TILES[1:]):
                    if i == 0:
                        pool.wait_ge(sums_ready, PRIME + h - 1)
                    pool.wait_ge(probs_ready, PRIME + h * (KT * QB) + QB * (kt + 1))
                    if i == 0:
                        one = probs[POOL_TILES[0] % PROBS]
                    else:
                        pool.wait_ge(pool_added, PRIME + h * POOL_ADDS + i)
                        one = total
                    nc.gpsimd.tensor_tensor(total[:], one[:], probs[kt % PROBS][:], ALU.add).then_inc(pool_added, 1)

            heads(pool, body)

        @block.scalar
        def _(act):
            for s in (probs_ready, pv_copied, sums_copied):
                act.sem_inc(s, PRIME)

            def exps(h, kt):
                for q in range(QB):
                    if q == 0:
                        act.wait_ge(tile_used, PRIME + h * KT + kt - PROBS + 1)
                        old, back = ((kt - PROBS), 0) if kt >= PROBS else (kt - PROBS + KT, 1)
                        if old in POOL_TILES:
                            act.wait_ge(pool_added, PRIME + h * POOL_ADDS - back * POOL_ADDS + adds_after(old))
                        if old in DVE_TILES:
                            act.wait_ge(dve_added, PRIME + h * DVE_CHUNKS - back * DVE_CHUNKS + chunks_after(old))
                    act.wait_ge(scores_ready, h * (KT * QB) + kt * QB + q + 1)
                    nc.scalar.activation(probs[kt % PROBS][:, q * BLK:(q + 1) * BLK],
                                         st_bank[:, place(kt * QB + q)], ACT.Exp,
                                         scale=SCALE).then_inc(probs_ready, 1)

            def copy_bank(h, r, bank, copies, ready, value, copied):
                act.wait_ge(ready, value)
                act.wait_ge(context_ready, PRIME + h - 1)
                nc.scalar.activation(copies[r % 2][:], bank[:], ACT.Copy).then_inc(copied, 1)

            def high(n, par):
                act.wait_ge(ctx_loaded[par], (n // 2) * DMA + DMA)
                act.wait_ge(res_ready, PRIME + n * JT - JT)
                nc.scalar.activation(ctx_hi[par], ctx_in[par], ACT.Copy).then_inc(hi_ready, 1)

            for kt in range(CUT):
                exps(0, kt)

            def body(h, r, more, following):
                for kt in range(CUT, KT):
                    exps(h, kt)
                if more == 0:
                    act.wait_ge(context_ready, PRIME + h)
                    high(0, 0)
                for kt in range(CUT):
                    if more:
                        exps(h + 1, kt)
                    if kt == 0:
                        copy_bank(h, r, pv_bank, pv_copy, tile_used, PRIME + h * KT + KT, pv_copied)
                        if more == 0:
                            high(1, 1)
                    if kt == DVE_SUM_KT:
                        copy_bank(h, r, sum_bank, sum_copy, sums_ready, PRIME + h + 1, sums_copied)

            heads(act, body)
            for n in range(2, 4):
                high(n, n % 2)
            block_pairs(act, lambda n, par, ahead: high(n + 2, par) if ahead else None)

        @block.vector
        def _(dve):
            dve.sem_inc(max_scores_read, PRIME)
            dve.sem_inc(context_ready, PRIME)
            dve.sem_inc(res_ready, PRIME)
            dve.sem_inc(row_max_ready, PRIME)
            for r in range(GROUP):
                nc.vector.memset(k_st[r][MROW:MROW + 1, :].bitcast(F32), 1.0).then_inc(consts_ready, 1)

            def negate(s):
                dve.wait_ge(turned_ready, s + 1)
                nc.vector.tensor_scalar(max_row[:], sum_bank[0:QT, 0:P], -1.0, None,
                                        ALU.mult).then_inc(max_row_ready, 1)

            def work(kind, n, h, r):
                if kind == "add":
                    i, q = divmod(n, QB)
                    cols = slice(q * BLK, (q + 1) * BLK)
                    kt = DVE_TILES[i + 1]
                    if n == 0:
                        dve.wait_ge(sums_ready, PRIME + h)
                    if q == 0:
                        dve.wait_ge(probs_ready, PRIME + h * UNITS + QB * (kt + 1))
                    if i and q == 0:
                        dve.wait_ge(dve_added, PRIME + h * DVE_CHUNKS + i * QB)
                    one = probs[DVE_TILES[0] % PROBS] if i == 0 else dve_sum
                    nc.vector.tensor_tensor(dve_sum[:, cols], one[:, cols], probs[kt % PROBS][:, cols],
                                            ALU.add).then_inc(dve_added, 1)
                elif kind == "recip":
                    dve.wait_ge(sums_loaded, h * DMA + DMA)
                    nc.vector.reciprocal(ratio_col[:], sums_col[:]).then_inc(recip_ready, 1)
                else:
                    dve.wait_ge(ratio_loaded, h * (QB * DMA) + QB * DMA)
                    dve.wait_ge(context_stored[r % 2], PRIME + (h // 2) * (CTX_DMAS * DMA))
                    nc.vector.tensor_tensor(ctx_out[r % 2][:], pv_copy[r % 2][:], ratio[:],
                                            ALU.mult).then_inc(context_ready, 1)

            def maxima(s, r, units=True, old=True, mid=True, new=True):
                for k in range(UNITS):
                    if k == TURN_UNIT and new:
                        negate(s - 1)
                    if units:
                        if k == 0:
                            dve.wait_ge(row_max_ready, PRIME + s)
                        dve.wait_ge(max_scores_ready, s * UNITS + k + 1)
                        nc.vector.tensor_reduce(part_max[:, k:k + 1], sm_bank[:, place(k)], AX.X,
                                                ALU.max).then_inc(max_scores_read, 1)
                    if mid and k in SUM_WORK:
                        work("add", SUM_WORK[k], s - 2, (r - 2) % GROUP)
                    if old and k == RECIP_UNIT:
                        work("recip", 0, s - 3, (r - 3) % GROUP)
                    if old and k == SCALE_UNIT:
                        work("scale", 0, s - 3, (r - 3) % GROUP)
                if units:
                    dve.wait_ge(max_scores_read, PRIME + s * UNITS + UNITS)
                    nc.vector.tensor_reduce(row_max[:], part_max[:].rearrange("p (q b) -> p q b", b=QB), AX.X,
                                            ALU.max).then_inc(row_max_ready, 1)

            dve.sem_inc(dve_added, PRIME)
            maxima(0, 0, old=False, mid=False, new=False)
            maxima(1, 1, old=False, mid=False)
            maxima(2, 2, old=False)

            def body(h, r, more, following):
                if more == 0:
                    low(0, 0)
                    low(1, 1)
                    dve.wait_ge(tile_used, PRIME + h * KT + KT)
                    results(0, 0)
                    work("recip", 0, h, r)
                    low(2, 0)
                    results(1, 1)
                    work("scale", 0, h, r)
                else:
                    maxima(following + 2, (r + 3) % GROUP, units=more >= 3, mid=more >= 1, new=more >= 2)

            def low(n, par):
                dve.wait_ge(hi_ready, n + 1)
                nc.vector.tensor_tensor(ctx_lo[par], ctx_in[par], ctx_hi[par].bitcast(F32),
                                        ALU.subtract).then_inc(lo_ready, 1)

            def results(n, par):
                dve.wait_ge(y_loaded[par], (n // 2) * DMA + DMA)
                dve.wait_ge(stored[par], PRIME + (n // 2) * DMA)
                for j in range(JT):
                    dve.wait_ge(bank_ready, n * JT + j + 1)
                    nc.vector.tensor_tensor(res[par][:, j], out_banks[j], y_in[par][:, j],
                                            ALU.add).then_inc(res_ready, 1)

            heads(dve, body)

            def output(n, par, ahead):
                if ahead or par == 0:
                    low(n + 1, 1 - par)
                results(n, par)

            block_pairs(dve, output)

        @block.tensor
        def _(pe):
            pe.sem_inc(tile_used, PRIME)
            pe.sem_inc(sums_ready, PRIME)
            pe.wait_ge(consts_ready, 2 + GROUP)

            def max_scores(s, r, k):
                q, b = divmod(k, QB)
                if k == 0:
                    pe.wait_ge(head_loaded[r], PRIME + (s // GROUP) * (HEAD_DMAS * DMA) + HEAD_DMAS * DMA)
                pe.wait_ge(max_scores_read, PRIME + s * UNITS + read_before(k))
                nc.tensor.matmul(sm_bank[:, place(k)], q_st[r][0:ROWS, q * P:(q + 1) * P],
                                 k_st[r][0:ROWS, b * BLK:(b + 1) * BLK], start=True,
                                 stop=True).then_inc(max_scores_ready, 1)

            def scores(h, r, kt, q):
                u = kt * QB + q
                if u == 0:
                    pe.wait_ge(row_loaded[r], PRIME + (h // GROUP) * DMA + DMA)
                pe.wait_ge(probs_ready, PRIME + h * UNITS + read_before(u))
                nc.tensor.matmul(st_bank[:, place(u)], k_st[r][0:ROWS + 1, kt * P:(kt + 1) * P],
                                 q_st[r][0:ROWS + 1, q * BLK:(q + 1) * BLK], start=True,
                                 stop=True).then_inc(scores_ready, 1)

            def spread(bank, left, right, start, stop):
                for q in range(QB):
                    last = nc.tensor.matmul(bank[q * DH:(q + 1) * DH, :], left, right[:, q * BLK:(q + 1) * BLK],
                                            start=start, stop=stop)
                return last

            def use(h, r, kt):
                if kt == 0:
                    pe.wait_ge(pv_copied, PRIME + h)
                pe.wait_ge(probs_ready, PRIME + h * (KT * QB) + QB * (kt + 1))
                tile = probs[kt % PROBS]
                last = spread(pv_bank, v_sb[r][:, kt], tile, kt == 0, kt == KT - 1)
                if kt in direct:
                    if kt == direct[0]:
                        final = isinstance(h, int) and h == ALL_HEADS - 1
                        pe.wait_ge(max_row_ready, h + 1 if final else h + 2)
                        if final:
                            pe.wait_ge(sums_copied, PRIME + h)
                    last = spread(sum_bank, ones[:], tile, kt == direct[0], False)
                last.then_inc(tile_used, 1)

            def add_partial(h, r, kt):
                if kt == POOL_SUM_KT:
                    pe.wait_ge(pool_added, PRIME + h * POOL_ADDS + POOL_ADDS)
                    spread(sum_bank, ones[:], pool_sum[r % 2], False, False)
                if kt == DVE_SUM_KT:
                    pe.wait_ge(dve_added, PRIME + h * DVE_CHUNKS + DVE_CHUNKS)
                    spread(sum_bank, ones[:], dve_sum, False, True).then_inc(sums_ready, 1)

            direct = [kt for kt in range(KT) if kt not in POOL_TILES + DVE_TILES]

            def turn_max(s):
                pe.wait_ge(row_max_ready, PRIME + s + 1)
                pe.wait_ge(sums_copied, PRIME + s - 1)
                nc.tensor.transpose(sum_bank[0:QT, 0:P], row_max[:], ident[:]).then_inc(turned_ready, 1)

            def step(h, r, kt, following, more, last):
                if kt < KT - AHEAD:
                    s, ahead, k0 = following, 1, PER_TILE * (kt + AHEAD)
                else:
                    s, ahead, k0 = following + 1, 2, PER_TILE * (kt - KT + AHEAD)
                for q in range(QB):
                    if more >= ahead:
                        max_scores(s, (r + ahead) % GROUP, k0 + q)
                    elif q == ST_BANKS and last:
                        use(*last)
                        last = None
                    scores(h, r, kt, q)
                if last:
                    use(*last)
                if kt == KT - AHEAD and more >= 1:
                    turn_max(following)

            for k in range(UNITS):
                max_scores(0, 0, k)
            for k in range(TURN_UNIT):
                max_scores(1, 1, k)
            turn_max(0)
            for k in range(TURN_UNIT, AHEAD * PER_TILE):
                max_scores(1, 1, k)
            for kt in range(CUT):
                step(0, 0, kt, 1, 2, (0, 0, kt - 1) if kt else None)

            def body(h, r, more, following):
                r1 = (r + 1) % GROUP
                for kt in range(CUT, KT):
                    step(h, r, kt, following, more, (h, r, kt - 1))
                for kt in range(CUT):
                    last = (following, r1, kt - 1) if kt else (h, r, KT - 1)
                    if more >= 1:
                        step(following, r1, kt, following + 1, more - 1, last)
                    elif kt == 0:
                        use(*last)
                    if more >= 1:
                        add_partial(h, r, kt)

            def output(n, par, ahead):
                pe.wait_ge(lo_ready, n + 1)
                for j in range(JT):
                    pe.wait_ge(res_ready, PRIME + n * JT + j - JT + 1)
                    three_passes(nc, out_banks[j], lambda c: ctx_hi[par][:, c, j * P:(j + 1) * P],
                                 lambda c: ctx_lo[par][:, c, j * P:(j + 1) * P], lambda c: wo_hi[:, c],
                                 lambda c: wo_lo[:, c]).then_inc(bank_ready, 1)

            heads(pe, body)
            pe.wait_ge(w_loaded, 2 * DMA)
            pe.wait_ge(max_row_ready, ALL_HEADS)
            output(0, 0, True)
            for kt in (POOL_SUM_KT, DVE_SUM_KT):
                add_partial(ALL_HEADS - 1, (ALL_HEADS - 1) % GROUP, kt)
            output(1, 1, True)
            block_pairs(pe, output)


def build_program(nc, x, w, out):
    x, out = x.flatten_outer_dims(), out.flatten_outer_dims()
    scratch = lambda name, shape: nc.dram_tensor(name, shape, F32, kind="Internal").ap()
    dram = {n: scratch(f"s_{n}", [BATCH * DIM, SEQ]) for n in ("q_hi", "q_lo", "k_hi", "k_lo", "ctx")}
    dram |= {n: scratch(f"s_{n}", [BATCH * SEQ, DIM]) for n in ("v", "y")}
    dram |= {n: scratch(f"s_{n}", [DIM, DIM]) for n in ("wo_hi", "wo_lo")}
    dram |= {n: scratch(f"s_{n}", [2, SEQ]) for n in ("sums", "ratio")}
    with ExitStack() as ctx:
        sb = lambda name, shape, dt=F32: ctx.enter_context(nc.sbuf_tensor(name, shape, dt))
        keep = {
            "ident": sb("ident", [P, P]), "ones": sb("ones", [P, DH]), "power": sb("power", [P, JT]),
            "qk_bias": sb("qk_bias", [P, 2, CT]), "row_bias": sb("row_bias", [P, 3, DIM]),
            "w_hi": sb("w_hi", [P, 4, CT, DIM], F32R), "w_lo": sb("w_lo", [P, 4, CT, DIM], F32R),
        }
        build_weights(nc, ctx, w, dram, keep)
        build_project(nc, x, dram, keep)
    build_attend(nc, dram, out)


_NAMES = {
    "x": "L0_attn_query", "q": "L0_attn_q_w", "q_b": "L0_attn_q_b", "k": "L0_attn_k_w", "k_b": "L0_attn_k_b",
    "v": "L0_attn_v_w", "v_b": "L0_attn_v_b", "o": "L0_attn_out_w", "o_b": "L0_attn_out_b",
    "w": "L0_ffn_weight", "a1": "L0_ffn_aux_weight1", "a2": "L0_ffn_aux_weight2", "ffn_b": "L0_ffn_bias",
}


def kernel(**inputs):
    import numpy as np
    import concourse.bacc as bacc
    from concourse.bass_utils import run_bass_kernel_spmd

    nc = bacc.Bacc("TRN2", target_bir_lowering=False, num_devices=1)
    arrays, given = {}, {}
    for short, name in _NAMES.items():
        a = np.ascontiguousarray(inputs[name])
        arrays[f"in_{short}"] = a
        given[short] = nc.dram_tensor(f"in_{short}", a.shape, mybir.dt.from_np(a.dtype), kind="ExternalInput").ap()
    x = given.pop("x")
    out = nc.dram_tensor("out_0", x.shape, F32, kind="ExternalOutput").ap()
    build_program(nc, x, given, out)
    r = run_bass_kernel_spmd(nc, [arrays], core_ids=[0])
    return r.results[0]["out_0"]
```
